# Optimizing a Trainium2 kernel written in Bass

```python
import numpy as np
import jax
import jax.numpy as jnp

def _softmax(x, axis=-1):
    return jax.nn.softmax(x, axis=axis)

def _gelu(x):
    return jax.nn.gelu(x, approximate=True)

def _silu(x):
    return jax.nn.silu(x)

def _sigmoid(x):
    return jax.nn.sigmoid(x)

def _layernorm(x, axis=-1, eps=1e-05):
    m = jnp.mean(x, axis=axis, keepdims=True)
    v = jnp.var(x, axis=axis, keepdims=True)
    return (x - m) / jnp.sqrt(v + eps)

def _scatter_add(tgt, idx, src, axis=0):
    return tgt.at[idx].add(src)

def _segment_sum(src, seg, n):
    return jax.ops.segment_sum(src, seg, n)
kernel_name = 'mk_dlrm_tower_d1_rec_r8_8651bb'

def setup_inputs(seed: int=0):
    np.random.seed(seed)
    _w = jnp.asarray

    def _rec_inputs():
        import jax
        import jax.numpy as jnp
        _tk = jax.random.key(seed)
        dense_ctx = jax.random.normal(jax.random.fold_in(_tk, 190), (1024, 16), jnp.float32)
        ids = jnp.stack([jax.random.randint(jax.random.fold_in(_tk, 200 + f), (1024,), 0, v, jnp.int32) for f, v in enumerate([12500, 1000, 1250, 125000, 1250, 125000, 1000, 12500, 125000, 1250, 12500, 1250, 1000, 1250, 1000, 125000, 1250, 1250, 1250, 12500, 1000, 1000, 1250, 1000, 1250, 1000, 125000, 1250, 125000, 12500, 1250, 12500])], axis=1)
        tbl_0 = 0.05 * jax.random.normal(jax.random.fold_in(_tk, 500 + 0), (12500, 32), jnp.float32)
        tbl_1 = 0.05 * jax.random.normal(jax.random.fold_in(_tk, 500 + 1), (1000, 32), jnp.float32)
        tbl_2 = 0.05 * jax.random.normal(jax.random.fold_in(_tk, 500 + 2), (1250, 32), jnp.float32)
        tbl_3 = 0.05 * jax.random.normal(jax.random.fold_in(_tk, 500 + 3), (125000, 32), jnp.float32)
        tbl_4 = 0.05 * jax.random.normal(jax.random.fold_in(_tk, 500 + 4), (1250, 32), jnp.float32)
        tbl_5 = 0.05 * jax.random.normal(jax.random.fold_in(_tk, 500 + 5), (125000, 32), jnp.float32)
        tbl_6 = 0.05 * jax.random.normal(jax.random.fold_in(_tk, 500 + 6), (1000, 32), jnp.float32)
        tbl_7 = 0.05 * jax.random.normal(jax.random.fold_in(_tk, 500 + 7), (12500, 32), jnp.float32)
        tbl_8 = 0.05 * jax.random.normal(jax.random.fold_in(_tk, 500 + 8), (125000, 32), jnp.float32)
        tbl_9 = 0.05 * jax.random.normal(jax.random.fold_in(_tk, 500 + 9), (1250, 32), jnp.float32)
        tbl_10 = 0.05 * jax.random.normal(jax.random.fold_in(_tk, 500 + 10), (12500, 32), jnp.float32)
        tbl_11 = 0.05 * jax.random.normal(jax.random.fold_in(_tk, 500 + 11), (1250, 32), jnp.float32)
        tbl_12 = 0.05 * jax.random.normal(jax.random.fold_in(_tk, 500 + 12), (1000, 32), jnp.float32)
        tbl_13 = 0.05 * jax.random.normal(jax.random.fold_in(_tk, 500 + 13), (1250, 32), jnp.float32)
        tbl_14 = 0.05 * jax.random.normal(jax.random.fold_in(_tk, 500 + 14), (1000, 32), jnp.float32)
        tbl_15 = 0.05 * jax.random.normal(jax.random.fold_in(_tk, 500 + 15), (125000, 32), jnp.float32)
        tbl_16 = 0.05 * jax.random.normal(jax.random.fold_in(_tk, 500 + 16), (1250, 32), jnp.float32)
        tbl_17 = 0.05 * jax.random.normal(jax.random.fold_in(_tk, 500 + 17), (1250, 32), jnp.float32)
        tbl_18 = 0.05 * jax.random.normal(jax.random.fold_in(_tk, 500 + 18), (1250, 32), jnp.float32)
        tbl_19 = 0.05 * jax.random.normal(jax.random.fold_in(_tk, 500 + 19), (12500, 32), jnp.float32)
        tbl_20 = 0.05 * jax.random.normal(jax.random.fold_in(_tk, 500 + 20), (1000, 32), jnp.float32)
        tbl_21 = 0.05 * jax.random.normal(jax.random.fold_in(_tk, 500 + 21), (1000, 32), jnp.float32)
        tbl_22 = 0.05 * jax.random.normal(jax.random.fold_in(_tk, 500 + 22), (1250, 32), jnp.float32)
        tbl_23 = 0.05 * jax.random.normal(jax.random.fold_in(_tk, 500 + 23), (1000, 32), jnp.float32)
        tbl_24 = 0.05 * jax.random.normal(jax.random.fold_in(_tk, 500 + 24), (1250, 32), jnp.float32)
        tbl_25 = 0.05 * jax.random.normal(jax.random.fold_in(_tk, 500 + 25), (1000, 32), jnp.float32)
        tbl_26 = 0.05 * jax.random.normal(jax.random.fold_in(_tk, 500 + 26), (125000, 32), jnp.float32)
        tbl_27 = 0.05 * jax.random.normal(jax.random.fold_in(_tk, 500 + 27), (1250, 32), jnp.float32)
        tbl_28 = 0.05 * jax.random.normal(jax.random.fold_in(_tk, 500 + 28), (125000, 32), jnp.float32)
        tbl_29 = 0.05 * jax.random.normal(jax.random.fold_in(_tk, 500 + 29), (12500, 32), jnp.float32)
        tbl_30 = 0.05 * jax.random.normal(jax.random.fold_in(_tk, 500 + 30), (1250, 32), jnp.float32)
        tbl_31 = 0.05 * jax.random.normal(jax.random.fold_in(_tk, 500 + 31), (12500, 32), jnp.float32)
        _rk = jax.random.fold_in(_tk, 7)
        W_top1 = 0.0606339 * jax.random.normal(jax.random.fold_in(_tk, 801), (272, 512), jnp.float32)
        W_top2 = 0.0441942 * jax.random.normal(jax.random.fold_in(_tk, 802), (512, 256), jnp.float32)
        W_top3 = 0.0625 * jax.random.normal(jax.random.fold_in(_tk, 803), (256, 1), jnp.float32)
        b_top1 = jnp.zeros((512,), jnp.float32)
        b_top2 = jnp.zeros((256,), jnp.float32)
        return (dense_ctx, ids, tbl_0, tbl_1, tbl_2, tbl_3, tbl_4, tbl_5, tbl_6, tbl_7, tbl_8, tbl_9, tbl_10, tbl_11, tbl_12, tbl_13, tbl_14, tbl_15, tbl_16, tbl_17, tbl_18, tbl_19, tbl_20, tbl_21, tbl_22, tbl_23, tbl_24, tbl_25, tbl_26, tbl_27, tbl_28, tbl_29, tbl_30, tbl_31, W_top1, b_top1, W_top2, b_top2, W_top3)
    dense_ctx, ids, tbl_0, tbl_1, tbl_2, tbl_3, tbl_4, tbl_5, tbl_6, tbl_7, tbl_8, tbl_9, tbl_10, tbl_11, tbl_12, tbl_13, tbl_14, tbl_15, tbl_16, tbl_17, tbl_18, tbl_19, tbl_20, tbl_21, tbl_22, tbl_23, tbl_24, tbl_25, tbl_26, tbl_27, tbl_28, tbl_29, tbl_30, tbl_31, W_top1, b_top1, W_top2, b_top2, W_top3 = _rec_inputs()

    def _L0_rec_setup():
        import jax, jax.numpy as jnp
        import numpy as np
        B, F, D = (512, 32, 32)
        LAYER_SIZE = [128, 128]

        def _cin_forward(inputs, filters):
            x0 = inputs
            prev = inputs
            outs = []
            for W in filters:
                z = jnp.einsum('bhd,bmd->bhmd', x0, prev)
                b, h, m, d = z.shape
                z = z.reshape(b, h * m, d)
                cur = jnp.einsum('bpd,pn->bnd', z, W[0])
                cur = jax.nn.relu(cur)
                prev = cur
                outs.append(cur)
            result = jnp.concatenate(outs, axis=1)
            return jnp.sum(result, axis=-1)
        key = jax.random.key(seed)
        k1, k2, k3 = jax.random.split(key, 3)
        inputs = jax.random.normal(k1, (B, F, D), dtype=jnp.float32)
        field_nums = [F] + LAYER_SIZE
        filter_0 = jax.random.normal(k2, (1, field_nums[0] * field_nums[0], field_nums[1]), dtype=jnp.float32) * 0.05
        filter_1 = jax.random.normal(k3, (1, field_nums[0] * field_nums[1], field_nums[2]), dtype=jnp.float32) * 0.05
        return {'inputs': inputs, 'filter_0': filter_0, 'filter_1': filter_1}
    _L0_rec_all = _L0_rec_setup()
    _L0_rec_in = {k: v for k, v in _L0_rec_all.items() if k in ('filter_0', 'filter_1')}
    del _L0_rec_all
    return {'dense_ctx': dense_ctx, 'ids': ids, 'tbl_0': tbl_0, 'tbl_1': tbl_1, 'tbl_2': tbl_2, 'tbl_3': tbl_3, 'tbl_4': tbl_4, 'tbl_5': tbl_5, 'tbl_6': tbl_6, 'tbl_7': tbl_7, 'tbl_8': tbl_8, 'tbl_9': tbl_9, 'tbl_10': tbl_10, 'tbl_11': tbl_11, 'tbl_12': tbl_12, 'tbl_13': tbl_13, 'tbl_14': tbl_14, 'tbl_15': tbl_15, 'tbl_16': tbl_16, 'tbl_17': tbl_17, 'tbl_18': tbl_18, 'tbl_19': tbl_19, 'tbl_20': tbl_20, 'tbl_21': tbl_21, 'tbl_22': tbl_22, 'tbl_23': tbl_23, 'tbl_24': tbl_24, 'tbl_25': tbl_25, 'tbl_26': tbl_26, 'tbl_27': tbl_27, 'tbl_28': tbl_28, 'tbl_29': tbl_29, 'tbl_30': tbl_30, 'tbl_31': tbl_31, 'W_top1': W_top1, 'b_top1': b_top1, 'W_top2': W_top2, 'b_top2': b_top2, 'W_top3': W_top3, 'L0_rec_filter_0': _L0_rec_in['filter_0'], 'L0_rec_filter_1': _L0_rec_in['filter_1']}

def reference(dense_ctx, ids, tbl_0, tbl_1, tbl_2, tbl_3, tbl_4, tbl_5, tbl_6, tbl_7, tbl_8, tbl_9, tbl_10, tbl_11, tbl_12, tbl_13, tbl_14, tbl_15, tbl_16, tbl_17, tbl_18, tbl_19, tbl_20, tbl_21, tbl_22, tbl_23, tbl_24, tbl_25, tbl_26, tbl_27, tbl_28, tbl_29, tbl_30, tbl_31, W_top1, b_top1, W_top2, b_top2, W_top3, L0_rec_filter_0, L0_rec_filter_1):
    import jax
    import jax.numpy as jnp

    def _L0_rec_ref(inputs, filter_0, filter_1):
        import jax, jax.numpy as jnp
        import numpy as np
        B, F, D = (512, 32, 32)
        LAYER_SIZE = [128, 128]

        def _cin_forward(inputs, filters):
            x0 = inputs
            prev = inputs
            outs = []
            for W in filters:
                z = jnp.einsum('bhd,bmd->bhmd', x0, prev)
                b, h, m, d = z.shape
                z = z.reshape(b, h * m, d)
                cur = jnp.einsum('bpd,pn->bnd', z, W[0])
                cur = jax.nn.relu(cur)
                prev = cur
                outs.append(cur)
            result = jnp.concatenate(outs, axis=1)
            return jnp.sum(result, axis=-1)
        return _cin_forward(inputs, (filter_0, filter_1))
    e = jnp.stack([tbl_0[ids[:, 0]], tbl_1[ids[:, 1]], tbl_2[ids[:, 2]], tbl_3[ids[:, 3]], tbl_4[ids[:, 4]], tbl_5[ids[:, 5]], tbl_6[ids[:, 6]], tbl_7[ids[:, 7]], tbl_8[ids[:, 8]], tbl_9[ids[:, 9]], tbl_10[ids[:, 10]], tbl_11[ids[:, 11]], tbl_12[ids[:, 12]], tbl_13[ids[:, 13]], tbl_14[ids[:, 14]], tbl_15[ids[:, 15]], tbl_16[ids[:, 16]], tbl_17[ids[:, 17]], tbl_18[ids[:, 18]], tbl_19[ids[:, 19]], tbl_20[ids[:, 20]], tbl_21[ids[:, 21]], tbl_22[ids[:, 22]], tbl_23[ids[:, 23]], tbl_24[ids[:, 24]], tbl_25[ids[:, 25]], tbl_26[ids[:, 26]], tbl_27[ids[:, 27]], tbl_28[ids[:, 28]], tbl_29[ids[:, 29]], tbl_30[ids[:, 30]], tbl_31[ids[:, 31]]], axis=1)
    z = _L0_rec_ref(e, L0_rec_filter_0, L0_rec_filter_1)
    z = z.reshape(z.shape[0], -1)
    h = jnp.concatenate([z, dense_ctx], axis=1)
    h = jnp.maximum(h @ W_top1 + b_top1, 0.0)
    h = jnp.maximum(h @ W_top2 + b_top2, 0.0)
    y = h @ W_top3
    return y

_drawn_inputs = setup_inputs


def setup_inputs(seed=0):
    import zlib

    import numpy as np

    out = dict(_drawn_inputs(seed))
    spreads = {'b_top1': (0.0, 0.426), 'b_top2': (0.0, 0.412)}
    factors = {'tbl_0': 5.575,
     'tbl_1': 6.019,
     'tbl_2': 5.885,
     'tbl_3': 6.074,
     'tbl_4': 6.343,
     'tbl_5': 5.765,
     'tbl_6': 6.131,
     'tbl_7': 6.396,
     'tbl_8': 5.988,
     'tbl_9': 6.133,
     'tbl_10': 5.968,
     'tbl_11': 5.864,
     'tbl_12': 5.838,
     'tbl_13': 6.121,
     'tbl_14': 6.063,
     'tbl_15': 5.815,
     'tbl_16': 6.246,
     'tbl_17': 5.862,
     'tbl_18': 6.176,
     'tbl_19': 6.338,
     'tbl_20': 5.936,
     'tbl_21': 5.935,
     'tbl_22': 5.795,
     'tbl_23': 6.044,
     'tbl_24': 6.127,
     'tbl_25': 5.907,
     'tbl_26': 5.914,
     'tbl_27': 6.077,
     'tbl_28': 5.969,
     'tbl_29': 6.123,
     'tbl_30': 6.313,
     'tbl_31': 6.008,
     'L0_rec_filter_1': 8.0}
    for name, (base, spread) in spreads.items():
        noise = np.random.default_rng([zlib.crc32(name.encode()), seed]).standard_normal(out[name].shape)
        drawn = base * np.exp(spread * noise) if base else spread * noise
        out[name] = jnp.asarray(drawn.astype(out[name].dtype))
    for name, factor in factors.items():
        out[name] = (out[name] * factor).astype(out[name].dtype)
    return out
```

```python
import concourse.bass as bass
from concourse import mybir
from contextlib import ExitStack

F32 = mybir.dt.float32
F32R = mybir.dt.float32r
U32 = mybir.dt.uint32
ALU = mybir.AluOpType
ACT = mybir.ActivationFunctionType
AX = mybir.AxisListType

P = 128
BATCH, FIELDS, DIM = 1024, 32, 32
TILES = BATCH // P
N1, N2 = 128, 128
DENSE = 16
HID1, HID2 = 512, 256
STEPS = 4
GROUPS = TILES * DIM // STEPS
GROUPS_PER_TILE = DIM // STEPS
COLS = STEPS * P
OFFSETS = FIELDS // 2 + 1
PAIRS = FIELDS * (FIELDS // 2) + FIELDS // 2
CHUNKS = -(-PAIRS // P)
ZCOLS = CHUNKS * P
XE = FIELDS + FIELDS // 2
BANKS = FIELDS * N2 // 512
HPB = 512 // N2
SLOTS = STEPS * BANKS
HALF = SLOTS // 2
HSTEP = BANKS // 2
RING_S, RING_V = 2, 4
V_AHEAD = RING_V * HPB
GATHERS_BY = [6, 6, 6, 6, 6, 2, 0, 0]


def count(per_group, g, event):
    pair, odd = g
    return pair * (2 * per_group) + (odd * per_group + event + 1)


def flat(g):
    return g[0] * 2 + g[1]


def is_first(g):
    return isinstance(g[0], int) and flat(g) == 0


def tile_of(group, most=TILES - 1):
    tile = group >> 3
    return tile if isinstance(tile, int) else tile.with_bounds(min_val=0, max_val=most)


def later(g, n):
    return (g[0], g[1] + n)


def dlrm_tower(nc, ids, dense, tables, w_top1, b_top1, w_top2, b_top2, w_top3, w0_a, w0_b, w1, out):
    ctx = ExitStack()
    with ctx:
        def sb(name, shape, dt=F32):
            return ctx.enter_context(nc.sbuf_tensor(name, shape, dt))

        def pb(name):
            return ctx.enter_context(nc.psum_tensor(name, [P, 512], F32))

        def sem(name):
            return ctx.enter_context(nc.semaphore(name))

        ids_sb = sb("ids_sb", [P, TILES, FIELDS], mybir.dt.int32)
        index = sb("index", [P, 2, FIELDS], mybir.dt.int32)
        emb = sb("emb", [P, 2, FIELDS, DIM])
        emb_d = emb[:, :, :, :].rearrange("p t f d -> p t d f")
        xe = sb("xe", [P, STEPS, XE])
        xs = sb("xs", [P, 2, STEPS, FIELDS])
        z = sb("z", [P, STEPS, ZCOLS])
        z_hi = sb("z_hi", [P, 2, COLS], F32R)
        z_lo = sb("z_lo", [P, 2, COLS], F32R)
        w0_sb = sb("w0_sb", [P, 2, CHUNKS, N1])
        w0_sum = sb("w0_sum", [P, CHUNKS, N1])
        w0_hi = sb("w0_hi", [P, CHUNKS, N1], F32R)
        w0_lo = sb("w0_lo", [P, CHUNKS, N1], F32R)
        w1_hi = sb("w1_hi", [P, FIELDS * N2], F32R)
        w1_lo = sb("w1_lo", [P, FIELDS * N2], F32R)
        p_hi = sb("p_hi", [P, 2, COLS], F32R)
        p_lo = sb("p_lo", [P, 2, COLS], F32R)
        scaled = sb("scaled", [P, 2, HSTEP * 512])
        part_s = sb("part_s", [P, 2, N2])
        part_v = sb("part_v", [P, 2, N2])
        both_v = sb("both_v", [P, N2])
        cur2 = sb("cur2", [P, N2])
        sum1 = sb("sum1", [P, TILES, COLS])
        sum2 = sb("sum2", [P, TILES + 1, N2])
        ident = sb("ident", [P, P])
        wt1 = sb("wt1", [P, 3, HID1])
        wt2 = sb("wt2", [P, HID1 // P, HID2])
        wt3 = sb("wt3", [P, HID2 // P])
        bt1 = sb("bt1", [P, HID1 // P])
        bt2 = sb("bt2", [P, HID2 // P])
        dense_sb = sb("dense_sb", [P, TILES, DENSE])
        h0 = sb("h0", [P, 3, BATCH])
        h1 = sb("h1", [P, HID1 // P, BATCH])
        h2 = sb("h2", [P, HID2 // P, BATCH])
        y_sb = sb("y_sb", [1, BATCH])
        w1_sb = scaled[:, :, :].rearrange("p a n -> p (a n)")

        zt_ps = pb("zt_ps")
        c_ps = pb("c_ps")
        gs_ps = [pb(f"gs_ps{i}") for i in range(RING_S)]
        gv_ps = [pb(f"gv_ps{i}") for i in range(RING_V)]
        tail_ps = [zt_ps, c_ps, *gs_ps, *gv_ps]

        ids_in = sem("ids_in")
        w0_in = sem("w0_in")
        w1_in = sem("w1_in")
        mlp_in = sem("mlp_in")
        out_done = sem("out_done")
        ident_ready = sem("ident_ready")
        index_ready = sem("index_ready")
        gathered = sem("gathered")
        w0_zeroed = sem("w0_zeroed")
        w0_summed = sem("w0_summed")
        w0_hi_ready = sem("w0_hi_ready")
        w0_ready = sem("w0_ready")
        w1_hi_ready = sem("w1_hi_ready")
        w1_ready = sem("w1_ready")
        xe_ready = sem("xe_ready")
        xs_ready = sem("xs_ready")
        z_ready = sem("z_ready")
        zt_ready = sem("zt_ready")
        z_hi_ready = sem("z_hi_ready")
        z_lo_ready = sem("z_lo_ready")
        chunk_done = sem("chunk_done")
        p_hi_ready = sem("p_hi_ready")
        p_lo_ready = sem("p_lo_ready")
        sum1_done = sem("sum1_done")
        gs_ready = sem("gs_ready")
        gv_ready = sem("gv_ready")
        gs_free = sem("gs_free")
        added = sem("added")
        both_ready = sem("both_ready")
        part_s_ready = sem("part_s_ready")
        tree = sem("tree")
        cur2_ready = sem("cur2_ready")
        sum2_done = sem("sum2_done")
        t_ready = sem("t_ready")
        h0_ready = sem("h0_ready")
        m1_done = sem("m1_done")
        h1_ready = sem("h1_ready")
        m2_done = sem("m2_done")
        h2_ready = sem("h2_ready")
        m3_done = sem("m3_done")
        y_ready = sem("y_ready")

        PAIRS_LOOPED = GROUPS // 2 - 1
        block = ctx.enter_context(nc.Block())

        @block.sync
        def _(sp):
            sp.dma_start(ids_sb[:, :, :], ids.rearrange("(t p) f -> p t f", p=P)).then_inc(ids_in, 16)
            full = (CHUNKS - 1) * P
            sp.wait_ge(w0_zeroed, 1)
            sp.dma_start(w0_sb[:, 0, 0:CHUNKS - 1, :],
                         w0_a[0:full, :].rearrange("(c p) n -> p c n", p=P)).then_inc(w0_in, 16)
            sp.dma_start(w0_sb[0:PAIRS - full, 0, CHUNKS - 1, :], w0_a[full:PAIRS, :]).then_inc(w0_in, 16)
            sp.dma_start(w0_sb[FIELDS:P, 1, 0, :], w0_b[FIELDS:P, :]).then_inc(w0_in, 16)
            sp.dma_start(w0_sb[:, 1, 1:CHUNKS - 1, :],
                         w0_b[P:full, :].rearrange("(c p) n -> p c n", p=P)).then_inc(w0_in, 16)
            sp.dma_start(w0_sb[0:PAIRS - full, 1, CHUNKS - 1, :], w0_b[full:PAIRS, :]).then_inc(w0_in, 16)
            sp.dma_start(w1_sb.rearrange("p (h n) -> p h n", n=N2),
                         w1.rearrange("(h m) n -> m h n", m=N1)).then_inc(w1_in, 16)
            sp.dma_start(dense_sb[:, :, :], dense.rearrange("(t p) k -> p t k", p=P)).then_inc(mlp_in, 16)
            sp.dma_start(wt1[:, 0:2, :], w_top1[0:2 * P, :].rearrange("(a p) n -> p a n", p=P)).then_inc(mlp_in, 16)
            sp.dma_start(wt1[0:DENSE, 2, :], w_top1[2 * P:2 * P + DENSE, :]).then_inc(mlp_in, 16)
            sp.dma_start(wt2[:, :, :], w_top2.rearrange("(a p) n -> p a n", p=P)).then_inc(mlp_in, 16)
            sp.dma_start(wt3[:, :], w_top3).then_inc(mlp_in, 16)
            sp.dma_start(bt1[:, :], b_top1).then_inc(mlp_in, 16)
            sp.dma_start(bt2[:, :], b_top2).then_inc(mlp_in, 16)
            sp.wait_ge(y_ready, 2)
            sp.dma_start(out.rearrange("b n -> n b"), y_sb[:, :]).then_inc(out_done, 16)
            sp.wait_ge(out_done, 16)

        MLP_IN = 7 * 16

        @block.gpsimd
        def _(pool):
            def take_index(tile, buf, after):
                if after is not None:
                    pool.wait_ge(gathered, after)
                pool.tensor_copy(index[:, buf, :], ids_sb[:, bass.ds(tile, 1), :].rearrange("p a f -> p (a f)"))\
                    .then_inc(index_ready, 1)

            def gather(field, buf):
                pool.indirect_dma_start(
                    out=emb[:, buf, field, :], out_offset=None, in_=tables[field],
                    in_offset=bass.IndirectOffsetOnAxis(ap=index[:, buf, field:field + 1].bitcast(U32), axis=0),
                ).then_inc(gathered, 16)

            def add_up(pair, step):
                n = pair * (2 * GROUPS_PER_TILE * STEPS) + step
                buf = step % 2
                pool.wait_ge(gs_free, n * HSTEP + HSTEP + RING_S)
                pool.tensor_tensor(scaled[:, buf, 0:1024], scaled[:, buf, 0:1024], scaled[:, buf, 1024:2048],
                                   ALU.add).then_inc(tree, 1)
                pool.wait_ge(tree, n * 3 + 1)
                pool.tensor_tensor(scaled[:, buf, 0:512], scaled[:, buf, 0:512], scaled[:, buf, 512:1024],
                                   ALU.add).then_inc(tree, 1)
                pool.wait_ge(tree, n * 3 + 2)
                pool.tensor_tensor(scaled[:, buf, 0:256], scaled[:, buf, 0:256], scaled[:, buf, 256:512],
                                   ALU.add).then_inc(tree, 1)
                pool.wait_ge(tree, n * 3 + 3)
                pool.wait_ge(cur2_ready, n + 1)
                pool.tensor_tensor(part_s[:, buf, :], scaled[:, buf, 0:128], scaled[:, buf, 128:256],
                                   ALU.add).then_inc(part_s_ready, 1)

            def two_tiles(pair, last):
                for odd in range(2):
                    more = not (last and odd)
                    for gt in range(GROUPS_PER_TILE):
                        if more and gt == 0:
                            tile = pair * 2 + odd
                            pool.wait_ge(xs_ready, tile * GROUPS_PER_TILE + 1)
                            take_index(tile + 1, 1 - odd, tile * (FIELDS * 16) + FIELDS * 16)
                            pool.wait_ge(index_ready, tile + 2)
                        add_up(pair, (odd * GROUPS_PER_TILE + gt) * STEPS)
                        if more:
                            at = sum(GATHERS_BY[:gt])
                            for field in range(at, at + GATHERS_BY[gt]):
                                gather(field, 1 - odd)
                        for c in range(1, STEPS):
                            add_up(pair, (odd * GROUPS_PER_TILE + gt) * STEPS + c)

            pool.wait_ge(ids_in, 16)
            take_index(0, 0, None)
            pool.wait_ge(index_ready, 1)
            for field in range(FIELDS):
                gather(field, 0)
            pool.memset(ident[:, :], 0.0).then_inc(ident_ready, 1)
            pool.wait_ge(ident_ready, 1)
            pool.affine_select(out=ident[:, :], in_=ident[:, :], compare_op=ALU.not_equal, fill=1.0,
                               base=0, pattern=[[-1, P]], channel_multiplier=1).then_inc(ident_ready, 1)
            pool.memset(part_s[:, :, :], 0.0).then_inc(part_s_ready, 2)
            with pool.Fori(0, TILES // 2 - 1) as pair:
                two_tiles(pair, False)
            two_tiles(TILES // 2 - 1, True)

        T_SLOT = [1 + 5 * k for k in range(CHUNKS)]
        HI_SLOT = T_SLOT
        LO_SLOT = [2 + 5 * k for k in range(CHUNKS)]
        M_SLOT = [5 + 5 * k for k in range(CHUNKS)]
        P_HI_SLOT, P_LO_SLOT = 26, 27
        XE_SLOT, XS_SLOT = 8, 16
        Z_SLOT = [23, 25, 29, 31]

        @block.scalar
        def _(act):
            def wait_xe(g):
                act.wait_ge(gathered, tile_of(flat(g)) * (FIELDS * 16) + FIELDS * 16)

            def copy_xe(g):
                tile, d = tile_of(flat(g)), (flat(g) & (GROUPS_PER_TILE - 1)) * STEPS
                src = emb_d[:, bass.ds(tile & 1, 1), bass.ds(d, STEPS), :].rearrange("p a d f -> p (a d) f")
                act.activation(xe[:, :, 0:FIELDS], src, ACT.Copy).then_inc(xe_ready, 1)
                act.activation(xe[:, :, FIELDS:XE], src[:, :, 0:XE - FIELDS], ACT.Copy).then_inc(xe_ready, 1)

            def copy_xs(g, buf):
                tile, d = tile_of(flat(g)), (flat(g) & (GROUPS_PER_TILE - 1)) * STEPS
                src = emb_d[:, bass.ds(tile & 1, 1), bass.ds(d, STEPS), :].rearrange("p a d f -> p (a d) f")
                act.activation(xs[:, buf, :, :], src, ACT.Copy).then_inc(xs_ready, 1)

            def high(g, k, buf):
                act.wait_ge(zt_ready, count(CHUNKS, g, k))
                if not (is_first(g) and k < 2):
                    act.wait_ge(chunk_done, count(CHUNKS, g, k - 2))
                act.activation(z_hi[:, buf, :], zt_ps[:, :], ACT.Copy).then_inc(z_hi_ready, 1)

            def relu_high(g, buf):
                act.wait_ge(chunk_done, count(CHUNKS, g, CHUNKS - 1))
                act.activation(p_hi[:, buf, :], c_ps[:, :], ACT.Relu).then_inc(p_hi_ready, 1)

            def scale_bank(g, c, q):
                i = c * HSTEP + q
                act.wait_ge(gs_ready, count(HALF, g, i))
                if q == 0:
                    act.wait_ge(part_s_ready, count(STEPS, g, c))
                for j in range(HPB):
                    h = 2 * q * HPB + j
                    last = act.activation(scaled[:, c % 2, (q * HPB + j) * N2:(q * HPB + j + 1) * N2],
                                          gs_ps[i % RING_S][:, j * N2:(j + 1) * N2], ACT.Copy,
                                          scale=xs[:, g[1] % 2, c, h:h + 1])
                last.then_inc(gs_free, 1)

            def period(g, layer1, prepare):
                nxt, par = later(g, 1), g[1]
                act.wait_ge(xs_ready, count(1, g, 0))
                for s in range(SLOTS):
                    if prepare and s == XE_SLOT:
                        act.wait_ge(z_ready, count(1, nxt, 0))
                        wait_xe(later(g, 2))
                    if layer1:
                        if s == XS_SLOT:
                            act.wait_ge(added, V_AHEAD + count(HALF * HPB, g, -1))
                        for k in range(CHUNKS):
                            if s == HI_SLOT[k]:
                                high(nxt, k, ((1 - par) * CHUNKS + k) % 2)
                        if s == P_HI_SLOT:
                            relu_high(nxt, 1 - par)
                    if s % 2 == 0:
                        scale_bank(g, s // BANKS, s % BANKS // 2)
                    if prepare and s == XE_SLOT:
                        copy_xe(later(g, 2))
                    if layer1 and s == XS_SLOT:
                        copy_xs(nxt, 1 - par)

            act.wait_ge(w0_summed, 1)
            act.activation(w0_hi[:, :, :], w0_sum[:, :, :], ACT.Copy).then_inc(w0_hi_ready, 1)
            act.wait_ge(w1_in, 16)
            act.activation(w1_hi[:, :], w1_sb, ACT.Copy).then_inc(w1_hi_ready, 1)
            zero = (0, 0)
            wait_xe(zero)
            copy_xe(zero)
            copy_xs(zero, 0)
            act.wait_ge(z_ready, 1)
            copy_xe((0, 1))
            for k in range(CHUNKS):
                high(zero, k, k % 2)
            relu_high(zero, 0)
            act.wait_ge(w1_ready, 1)
            with act.Fori(0, PAIRS_LOOPED) as pair:
                for par in range(2):
                    period((pair, par), True, True)
            period((PAIRS_LOOPED, 0), True, False)
            period((PAIRS_LOOPED, 1), False, False)
            act.wait_ge(t_ready, 4)
            for a in range(2):
                act.activation(h0[:, 1, a * 512:(a + 1) * 512], tail_ps[a][:, :], ACT.Copy).then_inc(h0_ready, 1)
                act.activation(h0[0:DENSE, 2, a * 512:(a + 1) * 512], tail_ps[2 + a][0:DENSE, :], ACT.Copy)\
                    .then_inc(h0_ready, 1)
            for o in range(HID1 // P):
                for a in range(2):
                    act.wait_ge(m1_done, o * 2 + a + 1)
                    act.activation(h1[:, o, a * 512:(a + 1) * 512], tail_ps[4 + (o * 2 + a) % 4][:, :], ACT.Relu,
                                   bias=bt1[:, o:o + 1]).then_inc(h1_ready, 1)
            for o in range(HID2 // P):
                for a in range(2):
                    act.wait_ge(m2_done, o * 2 + a + 1)
                    act.activation(h2[:, o, a * 512:(a + 1) * 512], tail_ps[o * 2 + a][:, :], ACT.Relu,
                                   bias=bt2[:, o:o + 1]).then_inc(h2_ready, 1)
            for a in range(2):
                act.wait_ge(m3_done, a + 1)
                act.activation(y_sb[:, a * 512:(a + 1) * 512], tail_ps[4 + a][0:1, :], ACT.Copy).then_inc(y_ready, 1)

        @block.vector
        def _(dve):
            def products(c):
                row = xe[:, c, 0:FIELDS]
                part = row.ap[0]
                here = bass.AP(row.tensor, row.offset, [part, [0, OFFSETS], [1, FIELDS]])
                beyond = bass.AP(row.tensor, row.offset, [part, [1, OFFSETS], [1, FIELDS]])
                to = z[:, c, 0:OFFSETS * FIELDS].rearrange("p (k h) -> p k h", h=FIELDS)
                return dve.tensor_tensor(to, here, beyond, ALU.mult)

            def low(g, k, buf):
                dve.wait_ge(z_hi_ready, count(CHUNKS, g, k))
                dve.tensor_tensor(z_lo[:, buf, :], zt_ps[:, :], z_hi[:, buf, :].bitcast(F32), ALU.subtract)\
                    .then_inc(z_lo_ready, 1)

            def relu_low(g, buf):
                dve.wait_ge(p_hi_ready, count(1, g, 0))
                dve.scalar_tensor_tensor(out=p_lo[:, buf, :], in0=c_ps[:, :], scalar=0.0,
                                         in1=p_hi[:, buf, :].bitcast(F32), op0=ALU.max, op1=ALU.subtract)\
                    .then_inc(p_lo_ready, 1)
                if not (is_first(g)):
                    dve.wait_ge(sum1_done, count(1, g, -1))
                total = sum1[:, bass.ds(tile_of(flat(g)), 1), :].rearrange("p a n -> p (a n)")
                dve.scalar_tensor_tensor(out=total, in0=c_ps[:, :], scalar=0.0, in1=total,
                                         op0=ALU.max, op1=ALU.add).then_inc(sum1_done, 1)

            def scale_and_add(g, c, q):
                i = c * HSTEP + q
                dve.wait_ge(gv_ready, count(HALF, g, i))
                for j in range(HPB):
                    n, h = q * HPB + j, (2 * q + 1) * HPB + j
                    src, run = gv_ps[i % RING_V][:, j * N2:(j + 1) * N2], part_v[:, n % 2, :]
                    by = xs[:, g[1] % 2, c, h:h + 1]
                    if n < 2:
                        if n == 0:
                            dve.wait_ge(both_ready, count(STEPS, g, c))
                        op = dve.tensor_scalar(run, src, by, None, ALU.mult)
                    else:
                        dve.wait_ge(added, V_AHEAD + count(HALF * HPB, g, c * HSTEP * HPB + n - 2))
                        op = dve.scalar_tensor_tensor(out=run, in0=src, scalar=by, in1=run,
                                                      op0=ALU.mult, op1=ALU.add)
                    op.then_inc(added, 1)

            def join(g, c):
                dve.wait_ge(added, V_AHEAD + count(HALF * HPB, g, (c + 1) * HSTEP * HPB - 1))
                dve.wait_ge(cur2_ready, count(STEPS, g, c) + 1)
                dve.tensor_tensor(both_v[:, :], part_v[:, 0, :], part_v[:, 1, :], ALU.add).then_inc(both_ready, 1)

            def finish(g, c):
                dve.wait_ge(both_ready, count(STEPS, g, c))
                dve.wait_ge(part_s_ready, count(STEPS, g, c) + 1)
                dve.wait_ge(sum2_done, count(STEPS, g, c))
                dve.tensor_tensor(cur2[:, :], both_v[:, :], part_s[:, (c + 1) % 2, :], ALU.add).then_inc(cur2_ready, 1)
                dve.wait_ge(cur2_ready, count(STEPS, g, c) + 1)
                tile = tile_of(flat(g) + (GROUPS_PER_TILE if c else GROUPS_PER_TILE - 1), TILES)
                total = sum2[:, bass.ds(tile, 1), :].rearrange("p a n -> p (a n)")
                dve.scalar_tensor_tensor(out=total, in0=cur2[:, :], scalar=0.0, in1=total,
                                         op0=ALU.max, op1=ALU.add).then_inc(sum2_done, 1)

            def period(g, layer1, prepare):
                nxt, par = later(g, 1), g[1]
                dve.wait_ge(xs_ready, count(1, g, 0))
                for s in range(SLOTS):
                    if layer1:
                        for k in range(CHUNKS):
                            if s == LO_SLOT[k]:
                                low(nxt, k, ((1 - par) * CHUNKS + k) % 2)
                        if s == P_LO_SLOT:
                            relu_low(nxt, 1 - par)
                    if prepare:
                        for c in range(STEPS):
                            if s == Z_SLOT[c]:
                                if c == 0:
                                    dve.wait_ge(xe_ready, count(2, later(g, 2), 1))
                                    dve.wait_ge(zt_ready, count(CHUNKS, nxt, CHUNKS - 1))
                                last = products(c)
                                if c == STEPS - 1:
                                    last.then_inc(z_ready, 1)
                    c, q = s // BANKS, s % BANKS // 2
                    if s % BANKS == BANKS - 1:
                        finish(g, c)
                    if s % 2:
                        scale_and_add(g, c, q)
                    if s % BANKS == BANKS - 1:
                        join(g, c)

            dve.memset(w0_sb[:, :, :, :], 0.0).then_inc(w0_zeroed, 1)
            dve.memset(z[:, :, OFFSETS * FIELDS:ZCOLS], 0.0).then_inc(gs_free, RING_S)
            dve.memset(part_v[:, :, :], 0.0).then_inc(added, V_AHEAD)
            dve.memset(sum1[:, :, :], 0.0)
            dve.memset(cur2[:, :], 0.0).then_inc(cur2_ready, 1)
            dve.memset(sum2[:, :, :], 0.0).then_inc(sum2_done, 1)
            dve.memset(both_v[:, :], 0.0).then_inc(both_ready, 1)
            dve.wait_ge(w0_in, 5 * 16)
            dve.tensor_tensor(w0_sum[:, :, :], w0_sb[:, 0, :, :], w0_sb[:, 1, :, :], ALU.add).then_inc(w0_summed, 1)
            dve.wait_ge(w0_hi_ready, 1)
            dve.tensor_tensor(w0_lo[:, :, :], w0_sum[:, :, :], w0_hi[:, :, :].bitcast(F32), ALU.subtract)\
                .then_inc(w0_ready, 1)
            dve.wait_ge(w1_hi_ready, 1)
            dve.tensor_tensor(w1_lo[:, :], w1_sb, w1_hi[:, :].bitcast(F32), ALU.subtract).then_inc(w1_ready, 1)
            dve.wait_ge(xe_ready, 2)
            for c in range(STEPS):
                last = products(c)
            last.then_inc(z_ready, 1)
            for k in range(CHUNKS):
                low((0, 0), k, k % 2)
            relu_low((0, 0), 0)
            dve.wait_ge(xe_ready, 4)
            dve.wait_ge(zt_ready, CHUNKS)
            for c in range(STEPS):
                last = products(c)
            last.then_inc(z_ready, 1)
            with dve.Fori(0, PAIRS_LOOPED) as pair:
                for par in range(2):
                    period((pair, par), True, True)
            period((PAIRS_LOOPED, 0), True, False)
            period((PAIRS_LOOPED, 1), False, False)
            finish((PAIRS_LOOPED, 1), STEPS)
            dve.wait_ge(sum1_done, GROUPS)
            dve.tensor_reduce(h0[:, 0, :].rearrange("p (t b) -> p t b", b=P),
                              sum1[:, :, :].rearrange("p t (c b) -> p t b c", b=P), AX.X, ALU.add).then_inc(h0_ready, 1)

        @block.tensor
        def _(pe):
            def transpose_chunk(g, k):
                if k == 0:
                    pe.wait_ge(z_ready, count(1, g, 0))
                if not (is_first(g) and k == 0):
                    pe.wait_ge(z_lo_ready, count(CHUNKS, g, k - 1))
                for c in range(STEPS):
                    last = pe.transpose(zt_ps[:, c * P:(c + 1) * P], z[:, c, k * P:(k + 1) * P], ident[:, :])
                last.then_inc(zt_ready, 1)

            def multiply_chunk(g, k, buf):
                if k == 0 and not (is_first(g)):
                    pe.wait_ge(sum1_done, count(1, g, -1))
                pe.wait_ge(z_lo_ready, count(CHUNKS, g, k))
                pe.matmul(c_ps[:, :], w0_hi[:, k, :], z_hi[:, buf, :], start=(k == 0), stop=False)
                pe.matmul(c_ps[:, :], w0_hi[:, k, :], z_lo[:, buf, :], start=False, stop=False)
                pe.matmul(c_ps[:, :], w0_lo[:, k, :], z_hi[:, buf, :], start=False, stop=(k == CHUNKS - 1))\
                    .then_inc(chunk_done, 1)

            def g_bank(g, s):
                c, q, i = s // BANKS, s % BANKS, s // 2
                ready, ring = (gv_ready, gv_ps) if s % 2 else (gs_ready, gs_ps)
                if s % 2:
                    pe.wait_ge(added, count(HALF * HPB, g, (i + 1) * HPB - 1))
                else:
                    pe.wait_ge(gs_free, count(HALF, g, i))
                to = ring[i % len(ring)][:, :]
                hi, lo = (p[:, g[1] % 2, c * P:(c + 1) * P] for p in (p_hi, p_lo))
                w_hi, w_lo = (w[:, q * 512:(q + 1) * 512] for w in (w1_hi, w1_lo))
                pe.matmul(to, hi, w_hi, start=True, stop=False)
                pe.matmul(to, hi, w_lo, start=False, stop=False)
                pe.matmul(to, lo, w_hi, start=False, stop=True).then_inc(ready, 1)

            def period(g, layer1):
                nxt, par = later(g, 1), g[1]
                pe.wait_ge(p_lo_ready, count(1, g, 0))
                for s in range(SLOTS):
                    if layer1:
                        for k in range(CHUNKS):
                            if s == M_SLOT[k]:
                                multiply_chunk(nxt, k, ((1 - par) * CHUNKS + k) % 2)
                            if s == T_SLOT[k]:
                                transpose_chunk(nxt, k)
                    g_bank(g, s)

            pe.wait_ge(ident_ready, 2)
            for k in range(CHUNKS):
                transpose_chunk((0, 0), k)
                if k == 0:
                    pe.wait_ge(w0_ready, 1)
                multiply_chunk((0, 0), k, k % 2)
            pe.wait_ge(w1_ready, 1)
            with pe.Fori(0, PAIRS_LOOPED) as pair:
                for par in range(2):
                    period((pair, par), True)
            period((PAIRS_LOOPED, 0), True)
            period((PAIRS_LOOPED, 1), False)
            pe.wait_ge(sum2_done, GROUPS * STEPS + 2)
            pe.wait_ge(gs_free, GROUPS * HALF + RING_S)
            pe.wait_ge(mlp_in, MLP_IN)
            for a in range(2):
                for t in range(4):
                    last = pe.transpose(tail_ps[a][:, t * P:(t + 1) * P], sum2[:, 1 + a * 4 + t, :], ident[:, :])
                last.then_inc(t_ready, 1)
                for t in range(4):
                    last = pe.transpose(tail_ps[2 + a][0:DENSE, t * P:(t + 1) * P], dense_sb[:, a * 4 + t, :],
                                        ident[:, :])
                last.then_inc(t_ready, 1)
            pe.wait_ge(h0_ready, 5)
            for o in range(HID1 // P):
                for a in range(2):
                    i = o * 2 + a
                    if i >= 4:
                        pe.wait_ge(h1_ready, i - 3)
                    cols = slice(a * 512, (a + 1) * 512)
                    to = tail_ps[4 + i % 4][:, :]
                    pe.matmul(to, wt1[:, 0, o * P:(o + 1) * P], h0[:, 0, cols], start=True, stop=False)
                    pe.matmul(to, wt1[:, 1, o * P:(o + 1) * P], h0[:, 1, cols], start=False, stop=False)
                    pe.matmul(to, wt1[0:DENSE, 2, o * P:(o + 1) * P], h0[0:DENSE, 2, cols], start=False, stop=True)\
                        .then_inc(m1_done, 1)
            pe.wait_ge(h1_ready, 8)
            for o in range(HID2 // P):
                for a in range(2):
                    for k in range(HID1 // P):
                        last = pe.matmul(tail_ps[o * 2 + a][:, :], wt2[:, k, o * P:(o + 1) * P],
                                         h1[:, k, a * 512:(a + 1) * 512], start=(k == 0), stop=(k == HID1 // P - 1))
                    last.then_inc(m2_done, 1)
            pe.wait_ge(h2_ready, 4)
            for a in range(2):
                for k in range(HID2 // P):
                    last = pe.matmul(tail_ps[4 + a][0:1, :], wt3[:, k:k + 1], h2[:, k, a * 512:(a + 1) * 512],
                                     start=(k == 0), stop=(k == HID2 // P - 1))
                last.then_inc(m3_done, 1)


def kernel(**inputs):
    import numpy as np
    import concourse.bacc as bacc
    from concourse.bass_utils import run_bass_kernel_spmd

    nc = bacc.Bacc("TRN2", target_bir_lowering=False, num_devices=1)
    arrays = {}

    def dram(name, a):
        a = np.ascontiguousarray(a)
        arrays[name] = a
        return nc.dram_tensor(name, a.shape, mybir.dt.from_np(a.dtype), kind="ExternalInput").ap()

    w0 = np.asarray(inputs["L0_rec_filter_0"])[0]
    pairs = [(h, (h + k) % FIELDS) for k in range(OFFSETS) for h in range(FIELDS)][:PAIRS]
    ids = dram("ids", inputs["ids"])
    dense = dram("dense_ctx", inputs["dense_ctx"])
    tables = [dram(f"tbl_{f}", inputs[f"tbl_{f}"]) for f in range(FIELDS)]
    w_top1, w_top2 = dram("W_top1", inputs["W_top1"]), dram("W_top2", inputs["W_top2"])
    b_top1, b_top2, w_top3 = (
        dram(n, np.asarray(inputs[n]).reshape(-1, P).T) for n in ("b_top1", "b_top2", "W_top3"))
    w0_a = dram("w0_a", w0[np.array([h * FIELDS + m for h, m in pairs])])
    w0_b = dram("w0_b", w0[np.array([m * FIELDS + h for h, m in pairs])])
    w1 = dram("w1", np.asarray(inputs["L0_rec_filter_1"])[0])
    out = nc.dram_tensor("y", (BATCH, 1), F32, kind="ExternalOutput").ap()
    dlrm_tower(nc, ids, dense, tables, w_top1, b_top1, w_top2, b_top2, w_top3, w0_a, w0_b, w1, out)
    r = run_bass_kernel_spmd(nc, [arrays], core_ids=[0])
    return r.results[0]["y"]
```

```python
import concourse.bass as bass
from concourse import mybir
from contextlib import ExitStack

F32 = mybir.dt.float32
F32R = mybir.dt.float32r
U32 = mybir.dt.uint32
ALU = mybir.AluOpType
ACT = mybir.ActivationFunctionType
AX = mybir.AxisListType

P = 128
BATCH, FIELDS, DIM = 1024, 32, 32
TILES = BATCH // P
N1, N2 = 128, 128
DENSE = 16
HID1, HID2 = 512, 256
STEPS = 4
GROUPS = TILES * DIM // STEPS
GROUPS_PER_TILE = DIM // STEPS
COLS = STEPS * P
OFFSETS = FIELDS // 2 + 1
PAIRS = FIELDS * (FIELDS // 2) + FIELDS // 2
FULL = FIELDS * (FIELDS // 2) // P
CHUNKS = FULL + 1
ORDER = [0, 1, 2, 4, 3]
ZCOLS = FULL * P
XE = FIELDS + FIELDS // 2
BANKS = FIELDS * N2 // 512
HPB = 512 // N2
SLOTS = STEPS * BANKS
PATTERN = ["SVSSVSVS", "VSVSVSVS"] * (STEPS // 2)
OWNER = "".join(PATTERN)
S_BANKS, V_BANKS = OWNER.count("S"), OWNER.count("V")
S_MOST = max(p.count("S") for p in PATTERN)
RING_S, RING_V = 2, 4
V_AHEAD = RING_V * HPB
TREE = [p.count("S") - 2 for p in PATTERN]
GATHERS_BY = [5, 5, 5, 6, 6, 5, 0, 0]


def count(per_group, g, event):
    pair, odd = g
    return pair * (2 * per_group) + (odd * per_group + event + 1)


def flat(g):
    return g[0] * 2 + g[1]


def is_first(g):
    return isinstance(g[0], int) and flat(g) == 0


def tile_of(group, most=TILES - 1):
    tile = group >> 3
    return tile if isinstance(tile, int) else tile.with_bounds(min_val=0, max_val=most)


def later(g, n):
    return (g[0], g[1] + n)


def own(s):
    return OWNER[:s].count(OWNER[s]), OWNER[s - s % BANKS:s].count(OWNER[s])


def dlrm_tower(nc, ids, dense, tables, w_top1, b_top1, w_top2, b_top2, w_top3, w0_a, w0_b, w1, out):
    ctx = ExitStack()
    with ctx:
        def sb(name, shape, dt=F32):
            return ctx.enter_context(nc.sbuf_tensor(name, shape, dt))

        def pb(name):
            return ctx.enter_context(nc.psum_tensor(name, [P, 512], F32))

        def sem(name):
            return ctx.enter_context(nc.semaphore(name))

        ids_sb = sb("ids_sb", [P, TILES, FIELDS], mybir.dt.int32)
        index = sb("index", [P, 2, FIELDS], mybir.dt.int32)
        emb = sb("emb", [P, 2, FIELDS, DIM])
        emb_d = emb[:, :, :, :].rearrange("p t f d -> p t d f")
        xe = sb("xe", [P, STEPS, XE])
        xs = sb("xs", [P, 2, STEPS, FIELDS])
        z = sb("z", [P, STEPS, ZCOLS])
        z_far = sb("z_far", [P, STEPS * FIELDS])
        z_hi = sb("z_hi", [P, 2, COLS], F32R)
        z_lo = sb("z_lo", [P, 2, COLS], F32R)
        w0_sb = sb("w0_sb", [P, 2, FULL + STEPS, N1])
        w0_sum = sb("w0_sum", [P, FULL + STEPS, N1])
        w0_hi = sb("w0_hi", [P, FULL + STEPS, N1], F32R)
        w0_lo = sb("w0_lo", [P, FULL + STEPS, N1], F32R)
        w1_hi = sb("w1_hi", [P, FIELDS * N2], F32R)
        w1_lo = sb("w1_lo", [P, FIELDS * N2], F32R)
        p_hi = sb("p_hi", [P, 2, COLS], F32R)
        p_lo = sb("p_lo", [P, 2, COLS], F32R)
        scaled = sb("scaled", [P, 2, S_MOST * 512])
        part_s = sb("part_s", [P, 2, STEPS, 2, N2])
        part_v = sb("part_v", [P, 2, STEPS, 2, N2])
        parts = sb("parts", [P, STEPS, 2, N2])
        cur2 = sb("cur2", [P, STEPS, N2])
        sum1 = sb("sum1", [P, TILES, COLS])
        sum2 = sb("sum2", [P, TILES + 1, STEPS * N2])
        ident = sb("ident", [P, P])
        wt1 = sb("wt1", [P, 3, HID1])
        wt2 = sb("wt2", [P, HID1 // P, HID2])
        wt3 = sb("wt3", [P, HID2 // P])
        bt1 = sb("bt1", [P, HID1 // P])
        bt2 = sb("bt2", [P, HID2 // P])
        dense_sb = sb("dense_sb", [P, TILES, DENSE])
        h0 = sb("h0", [P, 3, BATCH])
        y_sb = sb("y_sb", [1, BATCH])
        z2 = sb("z2", [P, TILES, N2])
        flat_scaled = scaled[:, :, :].rearrange("p a n -> p (a n)")
        w1_sb = flat_scaled[:, 0:FIELDS * N2]
        h1 = flat_scaled[:, 0:HID1 // P * BATCH].rearrange("p (o b) -> p o b", b=BATCH)
        h2 = z[:, :, :].rearrange("p c k -> p (c k)").rearrange("p (o b) -> p o b", b=BATCH)

        zt_ps = pb("zt_ps")
        c_ps = pb("c_ps")
        gs_ps = [pb(f"gs_ps{i}") for i in range(RING_S)]
        gv_ps = [pb(f"gv_ps{i}") for i in range(RING_V)]
        tail_ps = [zt_ps, c_ps, *gs_ps, *gv_ps]

        ids_in = sem("ids_in")
        w0_in = sem("w0_in")
        w1_in = sem("w1_in")
        mlp_in = sem("mlp_in")
        out_done = sem("out_done")
        ident_ready = sem("ident_ready")
        index_ready = sem("index_ready")
        gathered = sem("gathered")
        w0_zeroed = sem("w0_zeroed")
        w0_summed = sem("w0_summed")
        w0_hi_ready = sem("w0_hi_ready")
        w0_ready = sem("w0_ready")
        w1_hi_ready = sem("w1_hi_ready")
        w1_ready = sem("w1_ready")
        xe_ready = sem("xe_ready")
        xs_ready = sem("xs_ready")
        z_ready = sem("z_ready")
        zt_ready = sem("zt_ready")
        z_hi_ready = sem("z_hi_ready")
        z_lo_ready = sem("z_lo_ready")
        chunk_done = sem("chunk_done")
        p_hi_ready = sem("p_hi_ready")
        p_lo_ready = sem("p_lo_ready")
        sum1_done = sem("sum1_done")
        gs_ready = sem("gs_ready")
        gv_ready = sem("gv_ready")
        gs_free = sem("gs_free")
        added = sem("added")
        tree = sem("tree")
        folded = sem("folded")
        parts_ready = sem("parts_ready")
        cur2_ready = sem("cur2_ready")
        sum2_done = sem("sum2_done")
        z2_ready = sem("z2_ready")
        t_ready = sem("t_ready")
        h0_ready = sem("h0_ready")
        m1_done = sem("m1_done")
        h1_ready = sem("h1_ready")
        m2_done = sem("m2_done")
        h2_ready = sem("h2_ready")
        m3_done = sem("m3_done")
        y_ready = sem("y_ready")

        PAIRS_LOOPED = GROUPS // 2 - 1
        block = ctx.enter_context(nc.Block())

        @block.sync
        def _(sp):
            sp.dma_start(ids_sb[:, :, :], ids.rearrange("(t p) f -> p t f", p=P)).then_inc(ids_in, 16)
            sp.wait_ge(w0_zeroed, 1)
            sp.dma_start(w0_sb[:, 0, 0:FULL, :],
                         w0_a[0:ZCOLS, :].rearrange("(c p) n -> p c n", p=P)).then_inc(w0_in, 16)
            sp.dma_start(w0_sb[FIELDS:P, 1, 0, :], w0_b[FIELDS:P, :]).then_inc(w0_in, 16)
            sp.dma_start(w0_sb[:, 1, 1:FULL, :],
                         w0_b[P:ZCOLS, :].rearrange("(c p) n -> p c n", p=P)).then_inc(w0_in, 16)
            for c in range(STEPS):
                rows = slice(c * FIELDS, c * FIELDS + PAIRS - ZCOLS)
                sp.dma_start(w0_sb[rows, 0, FULL + c, :], w0_a[ZCOLS:PAIRS, :]).then_inc(w0_in, 16)
                sp.dma_start(w0_sb[rows, 1, FULL + c, :], w0_b[ZCOLS:PAIRS, :]).then_inc(w0_in, 16)
            sp.dma_start(w1_sb.rearrange("p (h n) -> p h n", n=N2),
                         w1.rearrange("(h m) n -> m h n", m=N1)).then_inc(w1_in, 16)
            sp.dma_start(dense_sb[:, :, :], dense.rearrange("(t p) k -> p t k", p=P)).then_inc(mlp_in, 16)
            sp.dma_start(wt1[:, 0:2, :], w_top1[0:2 * P, :].rearrange("(a p) n -> p a n", p=P)).then_inc(mlp_in, 16)
            sp.dma_start(wt1[0:DENSE, 2, :], w_top1[2 * P:2 * P + DENSE, :]).then_inc(mlp_in, 16)
            sp.dma_start(wt2[:, :, :], w_top2.rearrange("(a p) n -> p a n", p=P)).then_inc(mlp_in, 16)
            sp.dma_start(wt3[:, :], w_top3).then_inc(mlp_in, 16)
            sp.dma_start(bt1[:, :], b_top1).then_inc(mlp_in, 16)
            sp.dma_start(bt2[:, :], b_top2).then_inc(mlp_in, 16)
            sp.wait_ge(y_ready, 2)
            sp.dma_start(out.rearrange("b n -> n b"), y_sb[:, :]).then_inc(out_done, 16)
            sp.wait_ge(out_done, 16)

        MLP_IN = 7 * 16

        @block.gpsimd
        def _(pool):
            def take_index(tile, buf, after):
                if after is not None:
                    pool.wait_ge(gathered, after)
                pool.tensor_copy(index[:, buf, :], ids_sb[:, bass.ds(tile, 1), :].rearrange("p a f -> p (a f)"))\
                    .then_inc(index_ready, 1)

            def gather(field, buf):
                pool.indirect_dma_start(
                    out=emb[:, buf, field, :], out_offset=None, in_=tables[field],
                    in_offset=bass.IndirectOffsetOnAxis(ap=index[:, buf, field:field + 1].bitcast(U32), axis=0),
                ).then_inc(gathered, 16)

            def add_up(pair, group, c):
                g = pair * (2 * GROUPS_PER_TILE) + group
                buf, banks = scaled[:, c % 2, :], PATTERN[c].count("S")
                here = g * S_BANKS + RING_S + sum(p.count("S") for p in PATTERN[:c])
                done = g * sum(TREE) + sum(TREE[:c])
                pool.wait_ge(gs_free, here + 4)
                pool.tensor_tensor(buf[:, 0:1024], buf[:, 0:1024], buf[:, 1024:2048], ALU.add).then_inc(tree, 1)
                pool.wait_ge(tree, done + 1)
                pool.tensor_tensor(buf[:, 0:512], buf[:, 0:512], buf[:, 512:1024], ALU.add).then_inc(tree, 1)
                for b in range(4, banks):
                    pool.wait_ge(gs_free, here + b + 1)
                    pool.wait_ge(tree, done + b - 2)
                    pool.tensor_tensor(buf[:, 0:512], buf[:, 0:512], buf[:, b * 512:(b + 1) * 512],
                                       ALU.add).then_inc(tree, 1)
                if c == 0:
                    pool.wait_ge(parts_ready, g + 1)
                pool.wait_ge(tree, done + banks - 2)
                to = part_s[:, group % 2, c, :, :].rearrange("p a n -> p (a n)")
                pool.tensor_tensor(to, buf[:, 0:256], buf[:, 256:512], ALU.add).then_inc(folded, 1)

            def two_tiles(pair, last):
                for odd in range(2):
                    more = not (last and odd)
                    for gt in range(GROUPS_PER_TILE):
                        if more and gt == 0:
                            tile = pair * 2 + odd
                            pool.wait_ge(xs_ready, tile * GROUPS_PER_TILE + 1)
                            take_index(tile + 1, 1 - odd, tile * (FIELDS * 16) + FIELDS * 16)
                            pool.wait_ge(index_ready, tile + 2)
                        add_up(pair, odd * GROUPS_PER_TILE + gt, 0)
                        if more:
                            at = sum(GATHERS_BY[:gt])
                            for field in range(at, at + GATHERS_BY[gt]):
                                gather(field, 1 - odd)
                        for c in range(1, STEPS):
                            add_up(pair, odd * GROUPS_PER_TILE + gt, c)

            pool.wait_ge(ids_in, 16)
            take_index(0, 0, None)
            pool.wait_ge(index_ready, 1)
            for field in range(FIELDS):
                gather(field, 0)
            pool.memset(ident[:, :], 0.0).then_inc(ident_ready, 1)
            pool.wait_ge(ident_ready, 1)
            pool.affine_select(out=ident[:, :], in_=ident[:, :], compare_op=ALU.not_equal, fill=1.0,
                               base=0, pattern=[[-1, P]], channel_multiplier=1).then_inc(ident_ready, 1)
            pool.memset(part_s[:, :, :, :, :], 0.0).then_inc(folded, 2)
            with pool.Fori(0, TILES // 2 - 1) as pair:
                two_tiles(pair, False)
            two_tiles(TILES // 2 - 1, True)

        T_SLOT = [1, 6, 11, 16, 19]
        HI_SLOT = T_SLOT
        LO_SLOT = [t + 1 for t in T_SLOT]
        M_SLOT = [6, 11, 16, 19, 24]
        P_HI_SLOT, P_LO_SLOT = 25, 26
        XE_SLOT, XS_SLOT = 18, 9
        Z_SLOT = [22, 24]
        JOIN_SLOT = [9, 13, 20]

        @block.scalar
        def _(act):
            def wait_xe(g):
                act.wait_ge(gathered, tile_of(flat(g)) * (FIELDS * 16) + FIELDS * 16)

            def copy_xe(g):
                tile, d = tile_of(flat(g)), (flat(g) & (GROUPS_PER_TILE - 1)) * STEPS
                src = emb_d[:, bass.ds(tile & 1, 1), bass.ds(d, STEPS), :].rearrange("p a d f -> p (a d) f")
                act.activation(xe[:, :, 0:FIELDS], src, ACT.Copy).then_inc(xe_ready, 1)
                act.activation(xe[:, :, FIELDS:XE], src[:, :, 0:XE - FIELDS], ACT.Copy).then_inc(xe_ready, 1)

            def copy_xs(g, buf):
                tile, d = tile_of(flat(g)), (flat(g) & (GROUPS_PER_TILE - 1)) * STEPS
                src = emb_d[:, bass.ds(tile & 1, 1), bass.ds(d, STEPS), :].rearrange("p a d f -> p (a d) f")
                act.activation(xs[:, buf, :, :], src, ACT.Copy).then_inc(xs_ready, 1)

            def high(g, k, buf):
                cols = P if ORDER[k] == FULL else COLS
                act.wait_ge(zt_ready, count(CHUNKS, g, k))
                if not (is_first(g) and k < 2):
                    act.wait_ge(chunk_done, count(CHUNKS, g, k - 2))
                act.activation(z_hi[:, buf, 0:cols], zt_ps[:, 0:cols], ACT.Copy).then_inc(z_hi_ready, 1)

            def relu_high(g, buf):
                act.wait_ge(chunk_done, count(CHUNKS, g, CHUNKS - 1))
                act.activation(p_hi[:, buf, :], c_ps[:, :], ACT.Relu).then_inc(p_hi_ready, 1)

            def scale_bank(g, s):
                c, q = s // BANKS, s % BANKS
                i, at = own(s)
                if at == 0:
                    act.wait_ge(folded, count(STEPS, g, c))
                act.wait_ge(gs_ready, count(S_BANKS, g, i))
                bank = gs_ps[(g[1] % 2 * S_BANKS + i) % RING_S]
                for j in range(HPB):
                    h = q * HPB + j
                    last = act.activation(scaled[:, c % 2, (at * HPB + j) * N2:(at * HPB + j + 1) * N2],
                                          bank[:, j * N2:(j + 1) * N2], ACT.Copy,
                                          scale=xs[:, g[1] % 2, c, h:h + 1])
                last.then_inc(gs_free, 1)

            def period(g, layer1, prepare):
                nxt, par = later(g, 1), g[1]
                act.wait_ge(xs_ready, count(1, g, 0))
                for s in range(SLOTS):
                    if prepare and s == XE_SLOT:
                        act.wait_ge(z_ready, count(1, nxt, 0))
                        wait_xe(later(g, 2))
                    if layer1:
                        if s == XS_SLOT:
                            act.wait_ge(added, V_AHEAD + count(V_BANKS * HPB, g, -1))
                        for k in range(CHUNKS):
                            if s == HI_SLOT[k]:
                                high(nxt, k, ((1 - par) * CHUNKS + k) % 2)
                        if s == P_HI_SLOT:
                            relu_high(nxt, 1 - par)
                    if OWNER[s] == "S":
                        scale_bank(g, s)
                    if prepare and s == XE_SLOT:
                        copy_xe(later(g, 2))
                    if layer1 and s == XS_SLOT:
                        copy_xs(nxt, 1 - par)

            act.wait_ge(w0_summed, 1)
            act.activation(w0_hi[:, :, :], w0_sum[:, :, :], ACT.Copy).then_inc(w0_hi_ready, 1)
            act.wait_ge(w1_in, 16)
            act.activation(w1_hi[:, :], w1_sb, ACT.Copy).then_inc(w1_hi_ready, 1)
            zero = (0, 0)
            wait_xe(zero)
            copy_xe(zero)
            copy_xs(zero, 0)
            act.wait_ge(z_ready, 1)
            copy_xe((0, 1))
            for k in range(CHUNKS):
                high(zero, k, k % 2)
            relu_high(zero, 0)
            act.wait_ge(w1_ready, 1)
            with act.Fori(0, PAIRS_LOOPED) as pair:
                for par in range(2):
                    period((pair, par), True, True)
            period((PAIRS_LOOPED, 0), True, False)
            period((PAIRS_LOOPED, 1), False, False)
            act.wait_ge(t_ready, 4)
            for a in range(2):
                act.activation(h0[:, 1, a * 512:(a + 1) * 512], tail_ps[a][:, :], ACT.Copy).then_inc(h0_ready, 1)
                act.activation(h0[0:DENSE, 2, a * 512:(a + 1) * 512], tail_ps[2 + a][0:DENSE, :], ACT.Copy)\
                    .then_inc(h0_ready, 1)
            for o in range(HID1 // P):
                for a in range(2):
                    act.wait_ge(m1_done, o * 2 + a + 1)
                    act.activation(h1[:, o, a * 512:(a + 1) * 512], tail_ps[4 + (o * 2 + a) % 4][:, :], ACT.Relu,
                                   bias=bt1[:, o:o + 1]).then_inc(h1_ready, 1)
            for o in range(HID2 // P):
                for a in range(2):
                    act.wait_ge(m2_done, o * 2 + a + 1)
                    act.activation(h2[:, o, a * 512:(a + 1) * 512], tail_ps[o * 2 + a][:, :], ACT.Relu,
                                   bias=bt2[:, o:o + 1]).then_inc(h2_ready, 1)
            for a in range(2):
                act.wait_ge(m3_done, a + 1)
                act.activation(y_sb[:, a * 512:(a + 1) * 512], tail_ps[4 + a][0:1, :], ACT.Copy).then_inc(y_ready, 1)

        @block.vector
        def _(dve):
            def products(half):
                row = xe[:, 2 * half, 0:FIELDS]
                part = row.ap[0]
                here = bass.AP(row.tensor, row.offset, [part, [XE, 2], [0, OFFSETS - 1], [1, FIELDS]])
                beyond = bass.AP(row.tensor, row.offset, [part, [XE, 2], [1, OFFSETS - 1], [1, FIELDS]])
                to = z[:, 2 * half:2 * half + 2, :].rearrange("p c (k h) -> p c k h", h=FIELDS)
                return dve.tensor_tensor(to, here, beyond, ALU.mult)

            def far_products():
                return dve.tensor_tensor(z_far[:, :].rearrange("p (c h) -> p c h", h=FIELDS),
                                         xe[:, :, 0:FIELDS], xe[:, :, FIELDS // 2:XE], ALU.mult)

            def low(g, k, buf):
                cols = P if ORDER[k] == FULL else COLS
                dve.wait_ge(z_hi_ready, count(CHUNKS, g, k))
                dve.tensor_tensor(z_lo[:, buf, 0:cols], zt_ps[:, 0:cols], z_hi[:, buf, 0:cols].bitcast(F32),
                                  ALU.subtract).then_inc(z_lo_ready, 1)

            def relu_low(g, buf):
                dve.wait_ge(p_hi_ready, count(1, g, 0))
                dve.scalar_tensor_tensor(out=p_lo[:, buf, :], in0=c_ps[:, :], scalar=0.0,
                                         in1=p_hi[:, buf, :].bitcast(F32), op0=ALU.max, op1=ALU.subtract)\
                    .then_inc(p_lo_ready, 1)
                if not (is_first(g)):
                    dve.wait_ge(sum1_done, count(1, g, -1))
                total = sum1[:, bass.ds(tile_of(flat(g)), 1), :].rearrange("p a n -> p (a n)")
                dve.scalar_tensor_tensor(out=total, in0=c_ps[:, :], scalar=0.0, in1=total,
                                         op0=ALU.max, op1=ALU.add).then_inc(sum1_done, 1)

            def scale_and_add(g, s):
                c, q = s // BANKS, s % BANKS
                i, at = own(s)
                dve.wait_ge(gv_ready, count(V_BANKS, g, i))
                bank = gv_ps[(g[1] % 2 * V_BANKS + i) % RING_V]
                for j in range(HPB):
                    h = q * HPB + j
                    src, run = bank[:, j * N2:(j + 1) * N2], part_v[:, g[1] % 2, c, j % 2, :]
                    by = xs[:, g[1] % 2, c, h:h + 1]
                    if at == 0 and j < 2:
                        op = dve.tensor_scalar(run, src, by, None, ALU.mult)
                    else:
                        dve.wait_ge(added, V_AHEAD + count(V_BANKS * HPB, g, i * HPB + j - 2))
                        op = dve.scalar_tensor_tensor(out=run, in0=src, scalar=by, in1=run,
                                                      op0=ALU.mult, op1=ALU.add)
                    op.then_inc(added, 1)

            def join(g, stage):
                buf = (g[1] + 1) % 2
                if stage == 0:
                    dve.wait_ge(folded, count(STEPS, g, 0) + 1)
                    dve.wait_ge(added, V_AHEAD + count(V_BANKS * HPB, g, -1))
                    dve.tensor_tensor(parts[:, :, :, :], part_v[:, buf, :, :, :], part_s[:, buf, :, :, :],
                                      ALU.add).then_inc(parts_ready, 1)
                if stage == 1:
                    dve.wait_ge(parts_ready, count(1, g, 0) + 1)
                    dve.tensor_tensor(cur2[:, :, :], parts[:, :, 0, :], parts[:, :, 1, :], ALU.add)\
                        .then_inc(cur2_ready, 1)
                if stage == 2:
                    dve.wait_ge(cur2_ready, count(1, g, 0))
                    dve.wait_ge(sum2_done, count(1, g, 0))
                    tile = tile_of(flat(g) + GROUPS_PER_TILE - 1, TILES)
                    total = sum2[:, bass.ds(tile, 1), :].rearrange("p a n -> p (a n)")
                    dve.scalar_tensor_tensor(out=total, in0=cur2[:, :, :].rearrange("p c n -> p (c n)"), scalar=0.0,
                                             in1=total, op0=ALU.max, op1=ALU.add).then_inc(sum2_done, 1)

            def prepare_products(g):
                dve.wait_ge(xe_ready, count(2, g, 1))
                if not is_first(g):
                    dve.wait_ge(zt_ready, count(CHUNKS, g, -1))

            def period(g, layer1, prepare):
                nxt, par = later(g, 1), g[1]
                dve.wait_ge(xs_ready, count(1, g, 0))
                dve.wait_ge(parts_ready, count(1, g, 0))
                for s in range(SLOTS):
                    if layer1:
                        for k in range(CHUNKS):
                            if s == LO_SLOT[k]:
                                low(nxt, k, ((1 - par) * CHUNKS + k) % 2)
                        if s == P_LO_SLOT:
                            relu_low(nxt, 1 - par)
                    if prepare and s == Z_SLOT[0]:
                        prepare_products(later(g, 2))
                        products(0)
                        far_products()
                    if prepare and s == Z_SLOT[1]:
                        products(1).then_inc(z_ready, 1)
                    for stage in range(3):
                        if s == JOIN_SLOT[stage]:
                            join(g, stage)
                    if OWNER[s] == "V":
                        scale_and_add(g, s)

            dve.memset(w0_sb[:, :, :, :], 0.0).then_inc(w0_zeroed, 1)
            dve.memset(part_v[:, :, :, :, :], 0.0).then_inc(added, V_AHEAD)
            dve.memset(parts[:, :, :, :], 0.0).then_inc(parts_ready, 1)
            dve.memset(sum1[:, :, :], 0.0).then_inc(gs_free, RING_S)
            dve.memset(sum2[:, :, :], 0.0).then_inc(sum2_done, 1)
            dve.wait_ge(w0_in, (3 + 2 * STEPS) * 16)
            dve.tensor_tensor(w0_sum[:, :, :], w0_sb[:, 0, :, :], w0_sb[:, 1, :, :], ALU.add).then_inc(w0_summed, 1)
            dve.wait_ge(w0_hi_ready, 1)
            dve.tensor_tensor(w0_lo[:, :, :], w0_sum[:, :, :], w0_hi[:, :, :].bitcast(F32), ALU.subtract)\
                .then_inc(w0_ready, 1)
            dve.wait_ge(w1_hi_ready, 1)
            dve.tensor_tensor(w1_lo[:, :], w1_sb, w1_hi[:, :].bitcast(F32), ALU.subtract).then_inc(w1_ready, 1)
            for g in ((0, 0), (0, 1)):
                prepare_products(g)
                products(0)
                far_products()
                products(1).then_inc(z_ready, 1)
                if is_first(g):
                    for k in range(CHUNKS):
                        low(g, k, k % 2)
                    relu_low(g, 0)
            with dve.Fori(0, PAIRS_LOOPED) as pair:
                for par in range(2):
                    period((pair, par), True, True)
            period((PAIRS_LOOPED, 0), True, False)
            period((PAIRS_LOOPED, 1), False, False)
            for stage in range(3):
                join((PAIRS_LOOPED, 2), stage)
            dve.wait_ge(sum2_done, GROUPS + 2)
            dve.tensor_reduce(z2[:, :, :], sum2[:, 1:TILES + 1, :].rearrange("p t (c n) -> p t n c", n=N2),
                              AX.X, ALU.add).then_inc(z2_ready, 1)
            dve.wait_ge(sum1_done, GROUPS)
            dve.tensor_reduce(h0[:, 0, :].rearrange("p (t b) -> p t b", b=P),
                              sum1[:, :, :].rearrange("p t (c b) -> p t b c", b=P), AX.X, ALU.add).then_inc(h0_ready, 1)

        @block.tensor
        def _(pe):
            def transpose_chunk(g, k):
                if k == 0:
                    pe.wait_ge(z_ready, count(1, g, 0))
                if not (is_first(g) and k == 0):
                    pe.wait_ge(z_lo_ready, count(CHUNKS, g, k - 1))
                if ORDER[k] == FULL:
                    last = pe.transpose(zt_ps[:, 0:P], z_far[:, :], ident[:, :])
                else:
                    for c in range(STEPS):
                        last = pe.transpose(zt_ps[:, c * P:(c + 1) * P], z[:, c, ORDER[k] * P:(ORDER[k] + 1) * P],
                                            ident[:, :])
                last.then_inc(zt_ready, 1)

            def multiply_chunk(g, k, buf):
                if k == 0 and not is_first(g):
                    pe.wait_ge(sum1_done, count(1, g, -1))
                pe.wait_ge(z_lo_ready, count(CHUNKS, g, k))
                for n, (w, x) in enumerate(((w0_hi, z_hi), (w0_hi, z_lo), (w0_lo, z_hi))):
                    if ORDER[k] == FULL:
                        for c in range(STEPS):
                            last = pe.matmul(c_ps[:, c * P:(c + 1) * P], w[:, FULL + c, :], x[:, buf, 0:P],
                                             start=False, stop=False)
                    else:
                        last = pe.matmul(c_ps[:, :], w[:, ORDER[k], :], x[:, buf, :],
                                         start=(k == 0 and n == 0), stop=(k == CHUNKS - 1 and n == 2))
                last.then_inc(chunk_done, 1)

            def g_bank(g, s):
                c, q, (i, _) = s // BANKS, s % BANKS, own(s)
                if OWNER[s] == "V":
                    pe.wait_ge(added, count(V_BANKS * HPB, g, (i + 1) * HPB - 1))
                    to, ready = gv_ps[(g[1] % 2 * V_BANKS + i) % RING_V][:, :], gv_ready
                else:
                    pe.wait_ge(gs_free, count(S_BANKS, g, i))
                    to, ready = gs_ps[(g[1] % 2 * S_BANKS + i) % RING_S][:, :], gs_ready
                hi, lo = (p[:, g[1] % 2, c * P:(c + 1) * P] for p in (p_hi, p_lo))
                w_hi, w_lo = (w[:, q * 512:(q + 1) * 512] for w in (w1_hi, w1_lo))
                pe.matmul(to, hi, w_hi, start=True, stop=False)
                pe.matmul(to, hi, w_lo, start=False, stop=False)
                pe.matmul(to, lo, w_hi, start=False, stop=True).then_inc(ready, 1)

            def period(g, layer1):
                nxt, par = later(g, 1), g[1]
                pe.wait_ge(p_lo_ready, count(1, g, 0))
                for s in range(SLOTS):
                    if layer1:
                        for k in range(CHUNKS):
                            if s == M_SLOT[k]:
                                multiply_chunk(nxt, k, ((1 - par) * CHUNKS + k) % 2)
                            if s == T_SLOT[k]:
                                transpose_chunk(nxt, k)
                    g_bank(g, s)

            pe.wait_ge(ident_ready, 2)
            for k in range(CHUNKS):
                transpose_chunk((0, 0), k)
                if k == 0:
                    pe.wait_ge(w0_ready, 1)
                multiply_chunk((0, 0), k, k % 2)
            pe.wait_ge(w1_ready, 1)
            with pe.Fori(0, PAIRS_LOOPED) as pair:
                for par in range(2):
                    period((pair, par), True)
            period((PAIRS_LOOPED, 0), True)
            period((PAIRS_LOOPED, 1), False)
            pe.wait_ge(z2_ready, 1)
            pe.wait_ge(gs_free, GROUPS * S_BANKS + RING_S)
            pe.wait_ge(mlp_in, MLP_IN)
            for a in range(2):
                for t in range(4):
                    last = pe.transpose(tail_ps[a][:, t * P:(t + 1) * P], z2[:, a * 4 + t, :], ident[:, :])
                last.then_inc(t_ready, 1)
                for t in range(4):
                    last = pe.transpose(tail_ps[2 + a][0:DENSE, t * P:(t + 1) * P], dense_sb[:, a * 4 + t, :],
                                        ident[:, :])
                last.then_inc(t_ready, 1)
            pe.wait_ge(h0_ready, 5)
            for o in range(HID1 // P):
                for a in range(2):
                    i = o * 2 + a
                    if i >= 4:
                        pe.wait_ge(h1_ready, i - 3)
                    cols = slice(a * 512, (a + 1) * 512)
                    to = tail_ps[4 + i % 4][:, :]
                    pe.matmul(to, wt1[:, 0, o * P:(o + 1) * P], h0[:, 0, cols], start=True, stop=False)
                    pe.matmul(to, wt1[:, 1, o * P:(o + 1) * P], h0[:, 1, cols], start=False, stop=False)
                    pe.matmul(to, wt1[0:DENSE, 2, o * P:(o + 1) * P], h0[0:DENSE, 2, cols], start=False, stop=True)\
                        .then_inc(m1_done, 1)
            pe.wait_ge(h1_ready, 8)
            for o in range(HID2 // P):
                for a in range(2):
                    for k in range(HID1 // P):
                        last = pe.matmul(tail_ps[o * 2 + a][:, :], wt2[:, k, o * P:(o + 1) * P],
                                         h1[:, k, a * 512:(a + 1) * 512], start=(k == 0), stop=(k == HID1 // P - 1))
                    last.then_inc(m2_done, 1)
            pe.wait_ge(h2_ready, 4)
            for a in range(2):
                for k in range(HID2 // P):
                    last = pe.matmul(tail_ps[4 + a][0:1, :], wt3[:, k:k + 1], h2[:, k, a * 512:(a + 1) * 512],
                                     start=(k == 0), stop=(k == HID2 // P - 1))
                last.then_inc(m3_done, 1)


def kernel(**inputs):
    import numpy as np
    import concourse.bacc as bacc
    from concourse.bass_utils import run_bass_kernel_spmd

    nc = bacc.Bacc("TRN2", target_bir_lowering=False, num_devices=1)
    arrays = {}

    def dram(name, a):
        a = np.ascontiguousarray(a)
        arrays[name] = a
        return nc.dram_tensor(name, a.shape, mybir.dt.from_np(a.dtype), kind="ExternalInput").ap()

    w0 = np.asarray(inputs["L0_rec_filter_0"])[0]
    pairs = [(h, (h + k) % FIELDS) for k in range(OFFSETS) for h in range(FIELDS)][:PAIRS]
    ids = dram("ids", inputs["ids"])
    dense = dram("dense_ctx", inputs["dense_ctx"])
    tables = [dram(f"tbl_{f}", inputs[f"tbl_{f}"]) for f in range(FIELDS)]
    w_top1, w_top2 = dram("W_top1", inputs["W_top1"]), dram("W_top2", inputs["W_top2"])
    b_top1, b_top2, w_top3 = (
        dram(n, np.asarray(inputs[n]).reshape(-1, P).T) for n in ("b_top1", "b_top2", "W_top3"))
    w0_a = dram("w0_a", w0[np.array([h * FIELDS + m for h, m in pairs])])
    w0_b = dram("w0_b", w0[np.array([m * FIELDS + h for h, m in pairs])])
    w1 = dram("w1", np.asarray(inputs["L0_rec_filter_1"])[0])
    out = nc.dram_tensor("y", (BATCH, 1), F32, kind="ExternalOutput").ap()
    dlrm_tower(nc, ids, dense, tables, w_top1, b_top1, w_top2, b_top2, w_top3, w0_a, w0_b, w1, out)
    r = run_bass_kernel_spmd(nc, [arrays], core_ids=[0])
    return r.results[0]["y"]
```

```python
import concourse.bass as bass
from concourse import mybir
from contextlib import ExitStack

F32 = mybir.dt.float32
F32R = mybir.dt.float32r
U32 = mybir.dt.uint32
ALU = mybir.AluOpType
ACT = mybir.ActivationFunctionType
AX = mybir.AxisListType

P = 128
BATCH, FIELDS, DIM = 1024, 32, 32
TILES = BATCH // P
N1, N2 = 128, 128
DENSE = 16
ROWS = 32
HID1, HID2 = 512, 256
HALF = BATCH // 2
STEPS = 4
GROUPS = TILES * DIM // STEPS
GROUPS_PER_TILE = DIM // STEPS
COLS = STEPS * P
OFFSETS = FIELDS // 2 + 1
PAIRS = FIELDS * (FIELDS // 2) + FIELDS // 2
FULL = FIELDS * (FIELDS // 2) // P
CHUNKS = FULL + 1
ORDER = [0, 1, 2, 4, 3]
SHIFTS = P // FIELDS
SPLIT = [k for k in range(CHUNKS) if ORDER[k] != FULL]
ZCOLS = FULL * P
BANKS = FIELDS * N2 // 512
HPB = 512 // N2
SLOTS = STEPS * BANKS
PATTERN = ['VSSVSVSV', 'SVSSVSVS', 'SVVSVSVS', 'VSVSVVSS']
OWNER = "".join(PATTERN)
S_BANKS, V_BANKS = OWNER.count("S"), OWNER.count("V")
S_MOST = max(p.count("S") for p in PATTERN)
RING = 6
ROUNDS = [RING] * 5 + [RING - 1] + [RING] * 4 + [RING - 1]
BANK_OF = [bank for round_ in ROUNDS for bank in range(round_)]
assert len(BANK_OF) == 2 * SLOTS
S_AHEAD = RING
V_AHEAD = RING * HPB
TREE = [p.count("S") - 2 for p in PATTERN]
LOOKUP_STEPS = (GROUPS_PER_TILE - 2) * STEPS


def count(per_group, g, event):
    pair, odd = g
    return pair * (2 * per_group) + (odd * per_group + event + 1)


def flat(g):
    return g[0] * 2 + g[1]


def is_first(g):
    return isinstance(g[0], int) and flat(g) == 0


def tile_of(group, most=TILES - 1):
    tile = group >> 3
    return tile if isinstance(tile, int) else tile.with_bounds(min_val=0, max_val=most)


def later(g, n):
    return (g[0], g[1] + n)


def own(s):
    return OWNER[:s].count(OWNER[s]), OWNER[s - s % BANKS:s].count(OWNER[s])


def last_use(a):
    return max(b - back for b in range(2 * SLOTS) for back in (0, 2 * SLOTS)
               if BANK_OF[b] == BANK_OF[a] and b - back < a)


def dlrm_tower(nc, ids, dense, tables, w_top1, b_top1, w_top2, b_top2, w_top3, w0_a, w0_b, w1,
               x_rows, out):
    ctx = ExitStack()
    with ctx:
        def sb(name, shape, dt=F32):
            return ctx.enter_context(nc.sbuf_tensor(name, shape, dt))

        def pb(name):
            return ctx.enter_context(nc.psum_tensor(name, [P, 512], F32))

        def sem(name):
            return ctx.enter_context(nc.semaphore(name))

        ids_sb = sb("ids_sb", [P, TILES, FIELDS], mybir.dt.int32)
        index = sb("index", [P, 2, FIELDS], mybir.dt.int32)
        emb = sb("emb", [P, 2, FIELDS, DIM])
        emb_d = emb[:, :, :, :].rearrange("p t f d -> p t d f")
        xe = sb("xe", [P, STEPS, FIELDS])
        xt = sb("xt", [P, 2, P])
        x_here = sb("x_here", [P, 2, COLS])
        xs = sb("xs", [P, 2, STEPS, FIELDS])
        z = sb("z", [P, 2, FULL, COLS])
        z_far = sb("z_far", [P, 2, P])
        z_hi = sb("z_hi", [P, 2, COLS], F32R)
        z_lo = sb("z_lo", [P, 2, COLS], F32R)
        w0_sb = z[:, 1, :, :].rearrange("p a (b n) -> p (a b) n", n=N1).rearrange("p (w c) n -> p w c n", w=2)
        w0_sum = sb("w0_sum", [P, FULL + STEPS, N1])
        w0_hi = sb("w0_hi", [P, FULL, N1], F32R)
        w0_lo = sb("w0_lo", [P, FULL, N1], F32R)
        w1_hi = sb("w1_hi", [P, FIELDS * N2], F32R)
        w1_lo = sb("w1_lo", [P, FIELDS * N2], F32R)
        p_hi = sb("p_hi", [P, 2, COLS], F32R)
        p_lo = sb("p_lo", [P, 2, COLS], F32R)
        scaled = sb("scaled", [P, STEPS, S_MOST * 512])
        part_s = sb("part_s", [P, 2, STEPS, 2, N2])
        part_v = sb("part_v", [P, 2, STEPS, 2, N2])
        sum1 = sb("sum1", [P, TILES, COLS])
        sum2 = sb("sum2", [P, TILES + 1, STEPS * N2])
        ident = sb("ident", [P, P])
        wt1_hi = sb("wt1_hi", [P, 2, HID1], F32R)
        wt1_lo = sb("wt1_lo", [P, 2, HID1], F32R)
        wt2_hi = sb("wt2_hi", [P, HID1 // P, HID2], F32R)
        wt2_lo = sb("wt2_lo", [P, HID1 // P, HID2], F32R)
        wt3 = sb("wt3", [P, HID2 // P])
        bt1 = sb("bt1", [P, HID1 // P])
        bt2 = sb("bt2", [P, HID2 // P])
        dense_sb = sb("dense_sb", [P, TILES, DENSE])
        dense_hi = sb("dense_hi", [P, TILES, DENSE], F32R)
        dense_t3 = sb("dense_t3", [P, BATCH], F32R)
        wd_3 = sb("wd_3", [P, HID1], F32R)
        dense_3 = emb[:, 1, 0:3 * TILES * ROWS // DIM, :].rearrange("p f d -> p (f d)")\
            .rearrange("p (t a r) -> p t a r", a=3, r=ROWS)
        z1 = z[:, 1, 0:2, :].rearrange("p a n -> p (a n)")
        z2 = z[:, 1, 2:4, :].rearrange("p a (t n) -> p (a t) n", n=N2)
        y_sb = x_here[0:1, :, :].rearrange("p a n -> p (a n)")
        flat_scaled = scaled[:, :, :].rearrange("p a n -> p (a n)")
        w1_sb = flat_scaled[:, 0:FIELDS * N2]
        wd_sb = flat_scaled[:, FIELDS * N2:FIELDS * N2 + HID1]
        wt1_sb = z[:, 0, 0:2, :]
        wt2_sb = z[:, 0, 2:4, :].rearrange("p a (b n) -> p (a b) n", n=HID2)
        h1 = [emb[:, :, :, :].rearrange("p t f d -> p (t f d)").rearrange("p (o b) -> p o b", b=HALF),
              z[:, 0, :, :]]
        h1_hi, h1_lo = ([w[:, a * 4 * HALF:(a + 1) * 4 * HALF].rearrange("p (o b) -> p o b", b=HALF) for a in range(2)]
                        for w in (w1_hi, w1_lo))
        in_hi, in_lo = (z_hi, p_hi), (z_lo, p_lo)
        h2 = [z[:, 1, a * (HID2 // P):(a + 1) * (HID2 // P), :] for a in range(2)]

        xt_ps = pb("xt_ps")
        c_ps = pb("c_ps")
        g_ps = [pb(f"g_ps{i}") for i in range(RING)]
        y_ps = [c_ps, xt_ps]

        index0_in = sem("index0_in")
        ids_in = sem("ids_in")
        w0_in = sem("w0_in")
        w1_in = sem("w1_in")
        mlp_in = sem("mlp_in")
        out_done = sem("out_done")
        ident_ready = sem("ident_ready")
        index_ready = sem("index_ready")
        gathered = sem("gathered")
        w0_zeroed = sem("w0_zeroed")
        w0_summed = sem("w0_summed")
        w0_hi_ready = sem("w0_hi_ready")
        w0_ready = sem("w0_ready")
        w1_hi_ready = sem("w1_hi_ready")
        w1_ready = sem("w1_ready")
        xe_ready = sem("xe_ready")
        xt_made = sem("xt_made")
        xt_ready = sem("xt_ready")
        x_rows_out = sem("x_rows_out")
        x_here_in = [sem("x_here_in_even"), sem("x_here_in_odd")]
        x_there_in = [[sem(f"x_there_in_{parity}{k}") for k in range(CHUNKS)] for parity in ("even", "odd")]
        xs_ready = sem("xs_ready")
        z_ready = sem("z_ready")
        z_far_ready = sem("z_far_ready")
        z_hi_ready = sem("z_hi_ready")
        z_lo_ready = sem("z_lo_ready")
        chunk_done = sem("chunk_done")
        p_hi_ready = sem("p_hi_ready")
        p_lo_ready = sem("p_lo_ready")
        sum1_done = sem("sum1_done")
        gs_ready = sem("gs_ready")
        gv_ready = sem("gv_ready")
        gs_free = sem("gs_free")
        added = sem("added")
        tree = sem("tree")
        folded = sem("folded")
        parts_joined = sem("parts_joined")
        layer2_ready = sem("layer2_ready")
        sum2_done = sem("sum2_done")
        z2_ready = sem("z2_ready")
        z1_ready = sem("z1_ready")
        dense_3_ready = sem("dense_3_ready")
        dense_t = sem("dense_t")
        dense_ready = sem("dense_ready")
        z2_t = sem("z2_t")
        mlp_zeroed = sem("mlp_zeroed")
        dense_hi_ready = sem("dense_hi_ready")
        wd_hi_ready = sem("wd_hi_ready")
        wt_hi_ready = sem("wt_hi_ready")
        wt_ready = sem("wt_ready")
        in_hi_ready = sem("in_hi_ready")
        in_lo_ready = sem("in_lo_ready")
        m1_done = sem("m1_done")
        h1_ready = sem("h1_ready")
        h1_lo_ready = sem("h1_lo_ready")
        m2_done = sem("m2_done")
        h2_ready = sem("h2_ready")
        m3_done = sem("m3_done")
        y_ready = sem("y_ready")

        PAIRS_LOOPED = GROUPS // 2 - 1
        block = ctx.enter_context(nc.Block())

        order_in = {(0, 0): 1, (0, 1): 2, (1, 0): 3, (1, 1): 4}

        def chunk(par, k):
            return z_far[:, par, :] if ORDER[k] == FULL else z[:, par, ORDER[k], :]

        @block.sync
        def _(sp):
            def spread_x(g):
                sp.wait_ge(xt_ready, count(1, g, 0))
                par = g[1] % 2
                for turn in range(2):
                    rows = x_rows[par, turn * FIELDS:(turn + 1) * FIELDS, :].rearrange("f (c b) -> c f b", b=P)
                    sp.dma_start(rows, xt[:, par, :]).then_inc(x_rows_out, 16)
                sp.wait_ge(x_rows_out, count(2 * 16, g, 2 * 16 - 1))

                rows, fields = x_rows[par, :, :], [COLS, FIELDS]
                sp.dma_start(x_here[:, par, :], bass.AP(rows.tensor, rows.offset, [[0, SHIFTS], fields, [1, COLS]]))\
                    .then_inc(x_here_in[par], 16)
                for k in range(CHUNKS):
                    shift = ORDER[k] * SHIFTS
                    outer, columns = ([P, STEPS], P) if ORDER[k] == FULL else ([COLS, SHIFTS], COLS)
                    there = bass.AP(rows.tensor, rows.offset + shift * COLS, [outer, fields, [1, columns]])
                    sp.dma_start(chunk(par, k), there).then_inc(x_there_in[par][k], 16)

            sp.dma_start(index[:, 0, :], ids[0:P, :]).then_inc(index0_in, 16)
            sp.dma_start(ids_sb[:, :, :], ids.rearrange("(t p) f -> p t f", p=P)).then_inc(ids_in, 16)
            sp.wait_ge(w0_zeroed, 1)
            sp.dma_start(w0_sb[:, 0, 0:FULL, :],
                         w0_a[0:ZCOLS, :].rearrange("(c p) n -> p c n", p=P)).then_inc(w0_in, 16)
            sp.dma_start(w0_sb[FIELDS:P, 1, 0, :], w0_b[FIELDS:P, :]).then_inc(w0_in, 16)
            sp.dma_start(w0_sb[:, 1, 1:FULL, :],
                         w0_b[P:ZCOLS, :].rearrange("(c p) n -> p c n", p=P)).then_inc(w0_in, 16)
            for c in range(STEPS):
                rows = slice(c * FIELDS, c * FIELDS + PAIRS - ZCOLS)
                sp.dma_start(w0_sb[rows, 0, FULL + c, :], w0_a[ZCOLS:PAIRS, :]).then_inc(w0_in, 16)
                sp.dma_start(w0_sb[rows, 1, FULL + c, :], w0_b[ZCOLS:PAIRS, :]).then_inc(w0_in, 16)
            sp.dma_start(w1_sb.rearrange("p (h n) -> p h n", n=N2),
                         w1.rearrange("(h m) n -> m h n", m=N1)).then_inc(w1_in, 16)
            sp.dma_start(dense_sb[:, :, :], dense.rearrange("(t p) k -> p t k", p=P)).then_inc(mlp_in, 16)
            sp.dma_start(wt1_sb, w_top1[0:2 * P, :].rearrange("(a p) n -> p a n", p=P)).then_inc(mlp_in, 16)
            sp.wait_ge(mlp_zeroed, 1)
            for part in range(3):
                sp.dma_start(wd_sb[part * ROWS:part * ROWS + DENSE, :], w_top1[2 * P:2 * P + DENSE, :])\
                    .then_inc(mlp_in, 16)
            sp.dma_start(wt2_sb, w_top2.rearrange("(a p) n -> p a n", p=P)).then_inc(mlp_in, 16)
            sp.dma_start(wt3[:, :], w_top3).then_inc(mlp_in, 16)
            sp.dma_start(bt1[:, :], b_top1).then_inc(mlp_in, 16)
            sp.dma_start(bt2[:, :], b_top2).then_inc(mlp_in, 16)
            sp.wait_ge(wt_ready, 1)
            for g in ((0, 0), (0, 1)):
                spread_x(g)
            with sp.Fori(0, PAIRS_LOOPED) as pair:
                for par in range(2):
                    spread_x((pair, 2 + par))
            sp.wait_ge(y_ready, 2)
            sp.dma_start(out.rearrange("b n -> n b"), y_sb[:, :]).then_inc(out_done, 16)
            sp.wait_ge(out_done, 16)

        MLP_IN = 9 * 16

        @block.gpsimd
        def _(pool):
            def take_index(tile, buf, after):
                pool.wait_ge(gathered, after)
                pool.tensor_copy(index[:, buf, :], ids_sb[:, bass.ds(tile, 1), :].rearrange("p a f -> p (a f)"))\
                    .then_inc(index_ready, 1)

            def gather(field, buf):
                pool.indirect_dma_start(
                    out=emb[:, buf, field, :], out_offset=None, in_=tables[field],
                    in_offset=bass.IndirectOffsetOnAxis(ap=index[:, buf, field:field + 1].bitcast(U32), axis=0),
                ).then_inc(gathered, 16)

            def add_up(pair, group, c):
                g = pair * (2 * GROUPS_PER_TILE) + group
                buf, banks = scaled[:, c, :], PATTERN[c].count("S")
                here = g * S_BANKS + S_AHEAD + sum(p.count("S") for p in PATTERN[:c])
                done = g * sum(TREE) + sum(TREE[:c])
                pool.wait_ge(gs_free, here + 4)
                pool.tensor_tensor(buf[:, 0:1024], buf[:, 0:1024], buf[:, 1024:2048], ALU.add).then_inc(tree, 1)
                pool.wait_ge(tree, done + 1)
                pool.tensor_tensor(buf[:, 0:512], buf[:, 0:512], buf[:, 512:1024], ALU.add).then_inc(tree, 1)
                for b in range(4, banks):
                    pool.wait_ge(gs_free, here + b + 1)
                    pool.wait_ge(tree, done + b - 2)
                    pool.tensor_tensor(buf[:, 0:512], buf[:, 0:512], buf[:, b * 512:(b + 1) * 512],
                                       ALU.add).then_inc(tree, 1)
                if c == 0:
                    pool.wait_ge(parts_joined, g + 1)
                pool.wait_ge(tree, done + banks - 2)
                to = part_s[:, group % 2, c, :, :].rearrange("p a n -> p (a n)")
                pool.tensor_tensor(to, buf[:, 0:256], buf[:, 256:512], ALU.add).then_inc(folded, 1)

            def far_product(pair, group):
                par = group % 2
                pool.wait_ge(x_there_in[par][ORDER.index(FULL)], (pair * GROUPS_PER_TILE + (group // 2 + 1)) * 16)
                pool.tensor_tensor(z_far[:, par, :], xt[:, par, :], z_far[:, par, :], ALU.mult).then_inc(z_far_ready, 1)

            def two_tiles(pair, last):
                for odd in range(2):
                    more = not (last and odd)
                    for gt in range(GROUPS_PER_TILE):
                        if more and gt == 0:
                            tile = pair * 2 + odd
                            pool.wait_ge(xs_ready, tile * GROUPS_PER_TILE + 1)
                            take_index(tile + 1, 1 - odd, tile * (FIELDS * 16) + FIELDS * 16)
                            pool.wait_ge(index_ready, tile + 1)
                        if more or gt + 1 < GROUPS_PER_TILE:
                            far_product(pair, odd * GROUPS_PER_TILE + gt + 1)
                        for c in range(STEPS):
                            add_up(pair, odd * GROUPS_PER_TILE + gt, c)
                            if more:
                                start = FIELDS * (gt * STEPS + c) // LOOKUP_STEPS
                                end = FIELDS * (gt * STEPS + c + 1) // LOOKUP_STEPS
                                for field in range(start, min(end, FIELDS)):
                                    gather(field, 1 - odd)

            pool.memset(ident[:, :], 0.0).then_inc(ident_ready, 1)
            pool.wait_ge(ident_ready, 1)
            pool.affine_select(out=ident[:, :], in_=ident[:, :], compare_op=ALU.not_equal, fill=1.0,
                               base=0, pattern=[[-1, P]], channel_multiplier=1).then_inc(ident_ready, 1)
            pool.memset(part_s[:, :, :, :, :], 0.0).then_inc(folded, STEPS)
            pool.wait_ge(index0_in, 16)
            for field in range(FIELDS):
                gather(field, 0)
            pool.wait_ge(ids_in, 16)
            far_product(0, 0)
            with pool.Fori(0, TILES // 2 - 1) as pair:
                two_tiles(pair, False)
            two_tiles(TILES // 2 - 1, True)

        Z_SLOT = [1, 2, 6, 11]
        HI_SLOT = [4, 6, 8, 15]
        LO_SLOT = [4, 6, 9, 15]
        M_SLOT = [8, 11, 13, 16, 19]
        P_HI_SLOT, P_LO_SLOT = 19, 20
        SUM1_SLOT = 26
        XE_SLOT, XS_SLOT = 13, 8
        T_SLOT, XT_COPY_SLOT = 18, 18
        JOIN_SLOT = [9, 11, 17]
        Z2_SLOT, Z1_SLOT, Z2_T_SLOT = [3, 22], 6, 14
        IN1_SLOT, IN2_SLOT = (10, 12), (18, 20)

        @block.scalar
        def _(act):
            def wait_xe(g):
                act.wait_ge(gathered, tile_of(flat(g)) * (FIELDS * 16) + FIELDS * 16)

            def copy_xe(g):
                tile, d = tile_of(flat(g)), (flat(g) & (GROUPS_PER_TILE - 1)) * STEPS
                src = emb_d[:, bass.ds(tile & 1, 1), bass.ds(d, STEPS), :].rearrange("p a d f -> p (a d) f")
                act.activation(xe[:, :, :], src, ACT.Copy).then_inc(xe_ready, 1)

            def copy_xt(g):
                act.wait_ge(xt_made, count(1, g, 0))
                if not (isinstance(g[0], int) and flat(g) < 2):
                    act.wait_ge(chunk_done, count(CHUNKS, g, -CHUNKS - 1))
                act.activation(xt[:, g[1] % 2, :], xt_ps[:, 0:P], ACT.Copy).then_inc(xt_ready, 1)

            def copy_xs(g, buf):
                tile, d = tile_of(flat(g)), (flat(g) & (GROUPS_PER_TILE - 1)) * STEPS
                src = emb_d[:, bass.ds(tile & 1, 1), bass.ds(d, STEPS), :].rearrange("p a d f -> p (a d) f")
                act.activation(xs[:, buf, :, :], src, ACT.Copy).then_inc(xs_ready, 1)

            def high(g, i):
                k, before = SPLIT[i], SPLIT[i - 2] if i >= 2 else SPLIT[i - 2] - CHUNKS
                act.wait_ge(z_ready, count(FULL, g, i))
                if not (is_first(g) and i < 2):
                    act.wait_ge(chunk_done, count(CHUNKS, g, before))
                act.activation(z_hi[:, i % 2, :], chunk(g[1] % 2, k), ACT.Copy).then_inc(z_hi_ready, 1)

            def relu_high(g, buf):
                act.wait_ge(chunk_done, count(CHUNKS, g, CHUNKS - 1))
                act.activation(p_hi[:, buf, :], c_ps[:, :], ACT.Relu).then_inc(p_hi_ready, 1)

            def scale_bank(g, s):
                c, q = s // BANKS, s % BANKS
                i, at = own(s)
                if at == 0:
                    act.wait_ge(folded, count(STEPS, g, c))
                act.wait_ge(gs_ready, count(S_BANKS, g, i))
                bank = g_ps[BANK_OF[g[1] % 2 * SLOTS + s]]
                for j in range(HPB):
                    h = q * HPB + j
                    last = act.activation(scaled[:, c, (at * HPB + j) * N2:(at * HPB + j + 1) * N2],
                                          bank[:, j * N2:(j + 1) * N2], ACT.Copy,
                                          scale=xs[:, g[1] % 2, c, h:h + 1])
                last.then_inc(gs_free, 1)

            def input_high(a, layer):
                if layer == 0:
                    act.wait_ge(z1_ready, a + 1)
                else:
                    act.wait_ge(z2_t, a + 1)
                src = (z1[:, a * HALF:(a + 1) * HALF], xt_ps[:, :])[layer]
                act.activation(in_hi[a][:, layer, :], src, ACT.Copy).then_inc(in_hi_ready, 1)

            def period(g, layer1, prepare):
                nxt, par = later(g, 1), g[1]
                act.wait_ge(xs_ready, count(1, g, 0))
                for s in range(SLOTS):
                    if prepare and s == XE_SLOT:
                        act.wait_ge(xt_made, count(1, nxt, 0))
                        wait_xe(later(g, 2))
                    if layer1:
                        if s == XS_SLOT:
                            act.wait_ge(added, V_AHEAD + count(V_BANKS * HPB, g, -1))
                        for i in range(FULL):
                            if s == HI_SLOT[i]:
                                high(nxt, i)
                        if s == P_HI_SLOT:
                            relu_high(nxt, 1 - par)
                    if OWNER[s] == "S":
                        scale_bank(g, s)
                    if not layer1 and s == IN2_SLOT[0]:
                        input_high(0, 1)
                    if not layer1 and s == IN1_SLOT[0]:
                        input_high(0, 0)
                    if prepare and s == XE_SLOT:
                        copy_xe(later(g, 2))
                    if prepare and s == XT_COPY_SLOT:
                        copy_xt(later(g, 2))
                    if layer1 and s == XS_SLOT:
                        copy_xs(nxt, 1 - par)

            act.wait_ge(w0_summed, 1)
            act.activation(w0_hi[:, :, :], w0_sum[:, 0:FULL, :], ACT.Copy).then_inc(w0_hi_ready, 1)
            act.wait_ge(w1_in, 16)
            act.activation(w1_hi[:, :], w1_sb, ACT.Copy).then_inc(w1_hi_ready, 1)
            act.wait_ge(mlp_in, MLP_IN)
            act.activation(dense_hi[:, :, :], dense_sb[:, :, :], ACT.Copy).then_inc(dense_hi_ready, 1)
            act.activation(wd_3[0:3 * ROWS, :], wd_sb[0:3 * ROWS, :], ACT.Copy).then_inc(wd_hi_ready, 1)
            act.activation(wt1_hi[:, :, :], wt1_sb, ACT.Copy).then_inc(wt_hi_ready, 1)
            act.activation(wt2_hi[:, :, :], wt2_sb, ACT.Copy).then_inc(wt_hi_ready, 1)
            for a in range(2):
                act.wait_ge(dense_t, a + 1)
                act.activation(dense_t3[0:3 * ROWS, a * HALF:(a + 1) * HALF], g_ps[a][0:3 * ROWS, :], ACT.Copy)\
                    .then_inc(dense_ready, 1)
            zero = (0, 0)
            wait_xe(zero)
            copy_xe(zero)
            copy_xt(zero)
            copy_xs(zero, 0)
            copy_xe((0, 1))
            copy_xt((0, 1))
            for i in range(FULL):
                high(zero, i)
            relu_high(zero, 0)
            act.wait_ge(w1_ready, 1)
            with act.Fori(0, PAIRS_LOOPED) as pair:
                for par in range(2):
                    period((pair, par), True, True)
            period((PAIRS_LOOPED, 0), True, False)
            period((PAIRS_LOOPED, 1), False, False)
            input_high(1, 0)
            for a in range(2):
                if a:
                    input_high(1, 1)
                for o in range(HID1 // P):
                    act.wait_ge(m1_done, a * (HID1 // P) + o + 1)
                    act.activation(h1[a][:, o, :], g_ps[o][:, :], ACT.Relu, bias=bt1[:, o:o + 1]).then_inc(h1_ready, 1)
                    act.activation(h1_hi[a][:, o, :], g_ps[o][:, :], ACT.Relu, bias=bt1[:, o:o + 1])\
                        .then_inc(h1_ready, 1)
            for a in range(2):
                for o in range(HID2 // P):
                    act.wait_ge(m2_done, a * (HID2 // P) + o + 1)
                    act.activation(h2[a][:, o, :], g_ps[HID1 // P + o][:, :], ACT.Relu, bias=bt2[:, o:o + 1])\
                        .then_inc(h2_ready, 1)
            for a in range(2):
                act.wait_ge(m3_done, a + 1)
                act.activation(y_sb[:, a * HALF:(a + 1) * HALF], y_ps[a][0:1, :], ACT.Copy).then_inc(y_ready, 1)

        @block.vector
        def _(dve):
            def product(g, i):
                par, k = g[1] % 2, SPLIT[i]
                if i == 0:
                    dve.wait_ge(x_here_in[par], (g[0] + (g[1] // 2 + 1)) * 16)
                dve.wait_ge(x_there_in[par][k], (g[0] + (g[1] // 2 + 1)) * 16)
                dve.tensor_tensor(chunk(par, k), x_here[:, par, :], chunk(par, k), ALU.mult).then_inc(z_ready, 1)

            def low(g, i):
                dve.wait_ge(z_hi_ready, count(FULL, g, i))
                dve.tensor_tensor(z_lo[:, i % 2, :], chunk(g[1] % 2, SPLIT[i]), z_hi[:, i % 2, :].bitcast(F32),
                                  ALU.subtract).then_inc(z_lo_ready, 1)

            def relu_low(g, buf):
                dve.wait_ge(p_hi_ready, count(1, g, 0))
                dve.scalar_tensor_tensor(out=p_lo[:, buf, :], in0=c_ps[:, :], scalar=0.0,
                                         in1=p_hi[:, buf, :].bitcast(F32), op0=ALU.max, op1=ALU.subtract)\
                    .then_inc(p_lo_ready, 1)

            def add_sum1(g):
                if not (is_first(g)):
                    dve.wait_ge(sum1_done, count(1, g, -1))
                total = sum1[:, bass.ds(tile_of(flat(g)), 1), :].rearrange("p a n -> p (a n)")
                dve.scalar_tensor_tensor(out=total, in0=c_ps[:, :], scalar=0.0, in1=total,
                                         op0=ALU.max, op1=ALU.add).then_inc(sum1_done, 1)

            def scale_and_add(g, s):
                c, q = s // BANKS, s % BANKS
                i, at = own(s)
                dve.wait_ge(gv_ready, count(V_BANKS, g, i))
                bank = g_ps[BANK_OF[g[1] % 2 * SLOTS + s]]
                for j in range(HPB):
                    h = q * HPB + j
                    src, run = bank[:, j * N2:(j + 1) * N2], part_v[:, g[1] % 2, c, j % 2, :]
                    by = xs[:, g[1] % 2, c, h:h + 1]
                    if at == 0 and j < 2:
                        op = dve.tensor_scalar(run, src, by, None, ALU.mult)
                    else:
                        dve.wait_ge(added, V_AHEAD + count(V_BANKS * HPB, g, i * HPB + j - 2))
                        op = dve.scalar_tensor_tensor(out=run, in0=src, scalar=by, in1=run,
                                                      op0=ALU.mult, op1=ALU.add)
                    op.then_inc(added, 1)

            def join(g, stage):
                buf = (g[1] + 1) % 2
                mine, other = part_v[:, buf, :, 0, :], part_v[:, buf, :, 1, :]
                if stage == 0:
                    dve.wait_ge(folded, count(STEPS, g, -1) + STEPS)
                    dve.wait_ge(added, V_AHEAD + count(V_BANKS * HPB, g, -1))
                    dve.tensor_tensor(part_v[:, buf, :, :, :], part_v[:, buf, :, :, :], part_s[:, buf, :, :, :],
                                      ALU.add).then_inc(parts_joined, 1)
                if stage == 1:
                    dve.wait_ge(parts_joined, count(1, g, 0) + 1)
                    dve.tensor_tensor(mine, mine, other, ALU.add).then_inc(layer2_ready, 1)
                if stage == 2:
                    dve.wait_ge(layer2_ready, count(1, g, 0))
                    dve.wait_ge(sum2_done, count(1, g, 0))
                    tile = tile_of(flat(g) + GROUPS_PER_TILE - 1, TILES)
                    total = sum2[:, bass.ds(tile, 1), :].rearrange("p a (c n) -> p (a c) n", n=N2)
                    dve.scalar_tensor_tensor(out=total, in0=mine, scalar=0.0, in1=total, op0=ALU.max, op1=ALU.add)\
                        .then_inc(sum2_done, 1)

            def sum_z2(first, last):
                return dve.tensor_reduce(z2[:, first:last, :],
                                         sum2[:, 1 + first:1 + last, :].rearrange("p t (c n) -> p t n c", n=N2),
                                         AX.X, ALU.add)

            def sum_z1(first, last):
                return dve.tensor_reduce(z1[:, first * P:last * P].rearrange("p (t b) -> p t b", b=P),
                                         sum1[:, first:last, :].rearrange("p t (c b) -> p t b c", b=P), AX.X, ALU.add)

            def input_low(a, layer):
                dve.wait_ge(in_hi_ready, order_in[a, layer])
                src = (z1[:, a * HALF:(a + 1) * HALF], xt_ps[:, :])[layer]
                dve.tensor_tensor(in_lo[a][:, layer, :], src, in_hi[a][:, layer, :].bitcast(F32), ALU.subtract)\
                    .then_inc(in_lo_ready, 1)

            def period(g, layer1):
                nxt, par = later(g, 1), g[1]
                dve.wait_ge(xs_ready, count(1, g, 0))
                dve.wait_ge(sum2_done, count(1, g, 0))
                for s in range(SLOTS):
                    if layer1:
                        for i in range(FULL):
                            if s == Z_SLOT[i]:
                                product(nxt, i)
                            if s == LO_SLOT[i]:
                                low(nxt, i)
                        if s == P_LO_SLOT:
                            relu_low(nxt, 1 - par)
                        if s == SUM1_SLOT:
                            add_sum1(nxt)
                    for stage in range(3):
                        if s == JOIN_SLOT[stage]:
                            join(g, stage)
                    if not layer1:
                        if s == Z2_SLOT[0]:
                            dve.wait_ge(sum2_done, GROUPS)
                            sum_z2(0, TILES // 2).then_inc(z2_ready, 1)
                        if s == Z2_SLOT[1]:
                            sum_z2(TILES // 2, TILES - 1)
                        if s == Z1_SLOT:
                            dve.wait_ge(sum1_done, GROUPS)
                            sum_z1(0, TILES // 2).then_inc(z1_ready, 1)
                        for layer in range(2):
                            if s == (IN1_SLOT, IN2_SLOT)[layer][1]:
                                input_low(0, layer)
                    if OWNER[s] == "V":
                        scale_and_add(g, s)

            dve.memset(w0_sb[:, :, :, :], 0.0).then_inc(w0_zeroed, 1)
            dve.memset(wd_sb, 0.0).then_inc(mlp_zeroed, 1)
            dve.memset(dense_3[:, :, :, :], 0.0)
            dve.memset(part_v[:, :, :, :, :], 0.0).then_inc(added, V_AHEAD)
            dve.memset(sum1[:, 0:TILES // 2, :], 0.0).then_inc(parts_joined, 1)
            dve.memset(sum1[:, TILES // 2:TILES, :], 0.0).then_inc(gs_free, S_AHEAD)
            dve.memset(sum2[:, :, :], 0.0).then_inc(sum2_done, 1)
            dve.wait_ge(w0_in, (3 + 2 * STEPS) * 16)
            dve.tensor_tensor(w0_sum[:, :, :], w0_sb[:, 0, :, :], w0_sb[:, 1, :, :], ALU.add).then_inc(w0_summed, 1)
            dve.wait_ge(w0_hi_ready, 1)
            dve.tensor_tensor(w0_lo[:, :, :], w0_sum[:, 0:FULL, :], w0_hi[:, :, :].bitcast(F32), ALU.subtract)\
                .then_inc(w0_ready, 1)
            dve.wait_ge(dense_hi_ready, 1)
            dve.tensor_tensor(dense_3[:, :, 1, 0:DENSE], dense_sb[:, :, :], dense_hi[:, :, :].bitcast(F32),
                              ALU.subtract)
            for part in (0, 2):
                last = dve.tensor_copy(dense_3[:, :, part, 0:DENSE], dense_hi[:, :, :].bitcast(F32))
            last.then_inc(dense_3_ready, 1)
            dve.wait_ge(wd_hi_ready, 1)
            low_rows = slice(2 * ROWS, 3 * ROWS)
            dve.tensor_tensor(wd_3[low_rows, :], wd_sb[low_rows, :], wd_3[low_rows, :].bitcast(F32), ALU.subtract)
            dve.wait_ge(wt_hi_ready, 2)
            dve.tensor_tensor(wt1_lo[:, :, :], wt1_sb, wt1_hi[:, :, :].bitcast(F32), ALU.subtract)
            dve.tensor_tensor(wt2_lo[:, :, :], wt2_sb, wt2_hi[:, :, :].bitcast(F32), ALU.subtract)\
                .then_inc(wt_ready, 1)
            dve.wait_ge(w1_hi_ready, 1)
            dve.tensor_tensor(w1_lo[:, :], w1_sb, w1_hi[:, :].bitcast(F32), ALU.subtract).then_inc(w1_ready, 1)
            zero = (0, 0)
            product(zero, 0)
            for i in range(1, FULL):
                product(zero, i)
                low(zero, i - 1)
            low(zero, FULL - 1)
            relu_low(zero, 0)
            add_sum1(zero)
            with dve.Fori(0, PAIRS_LOOPED) as pair:
                for par in range(2):
                    period((pair, par), True)
            period((PAIRS_LOOPED, 0), True)
            period((PAIRS_LOOPED, 1), False)
            sum_z1(TILES // 2, TILES).then_inc(z1_ready, 1)
            for stage in range(3):
                join((PAIRS_LOOPED, 2), stage)
            dve.wait_ge(sum2_done, GROUPS + 2)
            sum_z2(TILES - 1, TILES).then_inc(z2_ready, 1)
            input_low(1, 0)
            for a in range(2):
                if a:
                    input_low(1, 1)
                for o in range(HID1 // P):
                    dve.wait_ge(h1_ready, 2 * (a * (HID1 // P) + o + 1))
                    dve.tensor_tensor(h1_lo[a][:, o, :], h1[a][:, o, :], h1_hi[a][:, o, :].bitcast(F32),
                                      ALU.subtract).then_inc(h1_lo_ready, 1)

        @block.tensor
        def _(pe):
            def transpose_x(g):
                pe.wait_ge(xe_ready, count(1, g, 0))
                if not is_first(g):
                    pe.wait_ge(xt_ready, count(1, g, -1))
                pe.transpose(xt_ps[:, 0:P], xe[:, :, :].rearrange("p c f -> p (c f)"), ident[:, :]).then_inc(xt_made, 1)

            def multiply_chunk(g, k):
                if k == 0 and not is_first(g):
                    pe.wait_ge(sum1_done, count(1, g, -1))
                if ORDER[k] == FULL:
                    pe.wait_ge(z_far_ready, count(1, g, 0))
                    for c in range(STEPS):
                        last = pe.matmul(c_ps[:, c * P:(c + 1) * P], w0_sum[:, FULL + c, :], z_far[:, g[1] % 2, :],
                                         start=False, stop=False)
                else:
                    i = SPLIT.index(k)
                    pe.wait_ge(z_lo_ready, count(FULL, g, i))
                    for n, (w, x) in enumerate(((w0_hi, z_hi), (w0_hi, z_lo), (w0_lo, z_hi))):
                        last = pe.matmul(c_ps[:, :], w[:, ORDER[k], :], x[:, i % 2, :],
                                         start=(k == 0 and n == 0), stop=(k == CHUNKS - 1 and n == 2))
                last.then_inc(chunk_done, 1)

            def g_bank(g, s):
                c, q, a = s // BANKS, s % BANKS, g[1] % 2 * SLOTS + s
                b = last_use(a)
                owner, n = OWNER[b % SLOTS], (OWNER * 2)[:b % (2 * SLOTS)].count(OWNER[b % SLOTS]) + 1
                if owner == "V":
                    n -= 2 * V_BANKS if b < 0 else 0
                    pe.wait_ge(added, g[0] * (2 * V_BANKS * HPB) + (V_AHEAD + n * HPB))
                else:
                    n -= 2 * S_BANKS if b < 0 else 0
                    pe.wait_ge(gs_free, g[0] * (2 * S_BANKS) + (S_AHEAD + n))
                to, ready = g_ps[BANK_OF[a]][:, :], gv_ready if OWNER[s] == "V" else gs_ready
                hi, lo = (p[:, g[1] % 2, c * P:(c + 1) * P] for p in (p_hi, p_lo))
                w_hi, w_lo = (w[:, q * 512:(q + 1) * 512] for w in (w1_hi, w1_lo))
                pe.matmul(to, hi, w_hi, start=True, stop=False)
                pe.matmul(to, hi, w_lo, start=False, stop=False)
                pe.matmul(to, lo, w_hi, start=False, stop=True).then_inc(ready, 1)

            def transpose_z2(a):
                pe.wait_ge(z2_ready, a + 1)
                if a:
                    pe.wait_ge(in_lo_ready, order_in[0, 1])
                for t in range(TILES // 2):
                    last = pe.transpose(xt_ps[:, t * P:(t + 1) * P], z2[:, a * TILES // 2 + t, :], ident[:, :])
                last.then_inc(z2_t, 1)

            def period(g, layer1, prepare):
                nxt, par = later(g, 1), g[1]
                pe.wait_ge(p_lo_ready, count(1, g, 0))
                for s in range(SLOTS):
                    if layer1:
                        for k in range(CHUNKS):
                            if s == M_SLOT[k]:
                                multiply_chunk(nxt, k)
                    if prepare and s == T_SLOT:
                        transpose_x(later(g, 2))
                    if not layer1 and s == Z2_T_SLOT:
                        transpose_z2(0)
                    g_bank(g, s)

            pe.wait_ge(ident_ready, 2)
            pe.wait_ge(dense_3_ready, 1)
            for a in range(2):
                for t in range(TILES // 2):
                    last = pe.transpose(g_ps[a][0:3 * ROWS, t * P:(t + 1) * P],
                                        dense_3[:, a * TILES // 2 + t, :, :].rearrange("p a k -> p (a k)"),
                                        ident[:, :])
                last.then_inc(dense_t, 1)
            for g in ((0, 0), (0, 1)):
                transpose_x(g)
            pe.wait_ge(w0_ready, 1)
            for k in range(CHUNKS):
                multiply_chunk((0, 0), k)
            pe.wait_ge(w1_ready, 1)
            pe.wait_ge(dense_ready, 2)
            with pe.Fori(0, PAIRS_LOOPED) as pair:
                for par in range(2):
                    period((pair, par), True, True)
            period((PAIRS_LOOPED, 0), True, False)
            period((PAIRS_LOOPED, 1), False, False)
            for a in range(2):
                cols = slice(a * HALF, (a + 1) * HALF)
                if a:
                    transpose_z2(a)
                for o in range(HID1 // P):
                    if a:
                        pe.wait_ge(h1_ready, 2 * (o + 1))
                    elif o == 0:
                        pe.wait_ge(added, V_AHEAD + GROUPS * V_BANKS * HPB)
                        pe.wait_ge(gs_free, S_AHEAD + GROUPS * S_BANKS)
                    to, w = g_ps[o][:, :], slice(o * P, (o + 1) * P)
                    pe.matmul(to, wd_3[0:3 * ROWS, w], dense_t3[0:3 * ROWS, cols], start=True, stop=False)
                    for layer in range(2):
                        if o == 0:
                            pe.wait_ge(in_lo_ready, order_in[a, layer])
                        hi, lo = in_hi[a][:, layer, :], in_lo[a][:, layer, :]
                        pe.matmul(to, wt1_hi[:, layer, w], hi, start=False, stop=False)
                        pe.matmul(to, wt1_hi[:, layer, w], lo, start=False, stop=False)
                        last = pe.matmul(to, wt1_lo[:, layer, w], hi, start=False, stop=(layer == 1))
                    last.then_inc(m1_done, 1)
            for a in range(2):
                for o in range(HID2 // P):
                    if a:
                        pe.wait_ge(h2_ready, o + 1)
                    for k in range(HID1 // P):
                        if o == 0:
                            pe.wait_ge(h1_lo_ready, a * (HID1 // P) + k + 1)
                        to, w = g_ps[HID1 // P + o][:, :], slice(o * P, (o + 1) * P)
                        pe.matmul(to, wt2_hi[:, k, w], h1_hi[a][:, k, :], start=(k == 0), stop=False)
                        pe.matmul(to, wt2_hi[:, k, w], h1_lo[a][:, k, :], start=False, stop=False)
                        last = pe.matmul(to, wt2_lo[:, k, w], h1_hi[a][:, k, :], start=False,
                                         stop=(k == HID1 // P - 1))
                    last.then_inc(m2_done, 1)
            for a in range(2):
                for k in range(HID2 // P):
                    pe.wait_ge(h2_ready, a * (HID2 // P) + k + 1)
                    last = pe.matmul(y_ps[a][0:1, :], wt3[:, k:k + 1], h2[a][:, k, :],
                                     start=(k == 0), stop=(k == HID2 // P - 1))
                last.then_inc(m3_done, 1)


def kernel(**inputs):
    import numpy as np
    import concourse.bacc as bacc
    from concourse.bass_utils import run_bass_kernel_spmd

    nc = bacc.Bacc("TRN2", target_bir_lowering=False, num_devices=1)
    arrays = {}

    def dram(name, a):
        a = np.ascontiguousarray(a)
        arrays[name] = a
        return nc.dram_tensor(name, a.shape, mybir.dt.from_np(a.dtype), kind="ExternalInput").ap()

    w0 = np.asarray(inputs["L0_rec_filter_0"])[0]
    pairs = [(h, (h + k) % FIELDS) for k in range(OFFSETS) for h in range(FIELDS)][:PAIRS]
    ids = dram("ids", inputs["ids"])
    dense = dram("dense_ctx", inputs["dense_ctx"])
    tables = [dram(f"tbl_{f}", inputs[f"tbl_{f}"]) for f in range(FIELDS)]
    w_top1, w_top2 = dram("W_top1", inputs["W_top1"]), dram("W_top2", inputs["W_top2"])
    b_top1, b_top2, w_top3 = (
        dram(n, np.asarray(inputs[n]).reshape(-1, P).T) for n in ("b_top1", "b_top2", "W_top3"))
    w0_a = dram("w0_a", w0[np.array([h * FIELDS + m for h, m in pairs])])
    w0_b = dram("w0_b", w0[np.array([m * FIELDS + h for h, m in pairs])])
    w1 = dram("w1", np.asarray(inputs["L0_rec_filter_1"])[0])
    x_rows = nc.dram_tensor("x_rows", (2, 2 * FIELDS, COLS), F32, kind="Internal").ap()
    out = nc.dram_tensor("y", (BATCH, 1), F32, kind="ExternalOutput").ap()
    dlrm_tower(nc, ids, dense, tables, w_top1, b_top1, w_top2, b_top2, w_top3, w0_a, w0_b, w1,
               x_rows, out)
    r = run_bass_kernel_spmd(nc, [arrays], core_ids=[0])
    return r.results[0]["y"]
```
